# Optimizing a Trainium2 kernel written in Bass

```python
import numpy as np
import jax
import jax.numpy as jnp

def _softmax(x, axis=-1):
    return jax.nn.softmax(x, axis=axis)

def _gelu(x):
    return jax.nn.gelu(x, approximate=True)

def _silu(x):
    return jax.nn.silu(x)

def _sigmoid(x):
    return jax.nn.sigmoid(x)

def _layernorm(x, axis=-1, eps=1e-05):
    m = jnp.mean(x, axis=axis, keepdims=True)
    v = jnp.var(x, axis=axis, keepdims=True)
    return (x - m) / jnp.sqrt(v + eps)

def _scatter_add(tgt, idx, src, axis=0):
    return tgt.at[idx].add(src)

def _segment_sum(src, seg, n):
    return jax.ops.segment_sum(src, seg, n)
kernel_name = 'mk_gnn_preln_d1_gnn_r64_d58f80'

def setup_inputs(seed: int=0):
    np.random.seed(seed)
    _w = jnp.asarray

    def _rec_inputs():
        import jax
        import jax.numpy as jnp
        _gk = jax.random.key(seed)
        x = -0.000202 + 1 * jax.random.normal(jax.random.fold_in(_gk, 1), (100000, 256), jnp.float32)
        src = jax.random.randint(jax.random.fold_in(_gk, 2), (25000,), 0, 100000, jnp.int32)
        dst = jax.random.randint(jax.random.fold_in(_gk, 3), (25000,), 0, 100000, jnp.int32)
        _o = jnp.argsort(dst, stable=True)
        src = src[_o]
        dst = dst[_o]
        edge_attr_64 = -5.3897e-05 + 0.999841 * jax.random.normal(jax.random.fold_in(_gk, 12), (25000, 64), jnp.float32)
        edge_weight1 = jax.random.uniform(jax.random.fold_in(_gk, 13), (25000, 1), jnp.float32, 0.0, 0.999998)
        return (x, src, dst, edge_attr_64, edge_weight1)
    x, src, dst, edge_attr_64, edge_weight1 = _rec_inputs()

    def _L0_gnn_setup():
        import jax, jax.numpy as jnp
        import numpy as np
        LOG2 = float(np.log(2.0))

        def ssp(x):
            return jax.nn.softplus(x) - LOG2
        N_ATOMS, N_EDGES, N_HF, N_RBF = (25000, 6250, 256, 64)
        key = jax.random.key(seed)
        ks = jax.random.split(key, 16)
        s = 1.0 / np.sqrt(N_HF)
        sr = 1.0 / np.sqrt(N_RBF)
        return {'x': jax.random.normal(ks[0], (N_ATOMS, N_HF), jnp.float32), 'rbf': jax.random.normal(ks[1], (N_EDGES, N_RBF), jnp.float32), 'dist_cut': jax.random.uniform(ks[2], (N_EDGES, 1), jnp.float32), 'idx_i': jax.random.randint(ks[3], (N_EDGES,), 0, N_ATOMS), 'idx_j': jax.random.randint(ks[4], (N_EDGES,), 0, N_ATOMS), 'W_in2f': jax.random.normal(ks[5], (N_HF, N_HF), jnp.float32) * s, 'Wf1': jax.random.normal(ks[6], (N_RBF, N_HF), jnp.float32) * sr, 'bf1': jnp.zeros((N_HF,), jnp.float32), 'Wf2': jax.random.normal(ks[7], (N_HF, N_HF), jnp.float32) * s, 'bf2': jnp.zeros((N_HF,), jnp.float32), 'Wo1': jax.random.normal(ks[8], (N_HF, N_HF), jnp.float32) * s, 'bo1': jnp.zeros((N_HF,), jnp.float32), 'Wo2': jax.random.normal(ks[9], (N_HF, N_HF), jnp.float32) * s, 'bo2': jnp.zeros((N_HF,), jnp.float32)}
    _L0_gnn_all = _L0_gnn_setup()
    _L0_gnn_in = {k: v for k, v in _L0_gnn_all.items() if k in ('W_in2f', 'Wf1', 'bf1', 'Wf2', 'bf2', 'Wo1', 'bo1', 'Wo2', 'bo2')}
    del _L0_gnn_all
    return {'x': x, 'src': src, 'dst': dst, 'edge_attr_64': edge_attr_64, 'edge_weight1': edge_weight1, 'L0_gnn_W_in2f': _L0_gnn_in['W_in2f'], 'L0_gnn_Wf1': _L0_gnn_in['Wf1'], 'L0_gnn_bf1': _L0_gnn_in['bf1'], 'L0_gnn_Wf2': _L0_gnn_in['Wf2'], 'L0_gnn_bf2': _L0_gnn_in['bf2'], 'L0_gnn_Wo1': _L0_gnn_in['Wo1'], 'L0_gnn_bo1': _L0_gnn_in['bo1'], 'L0_gnn_Wo2': _L0_gnn_in['Wo2'], 'L0_gnn_bo2': _L0_gnn_in['bo2']}

def reference(x, src, dst, edge_attr_64, edge_weight1, L0_gnn_W_in2f, L0_gnn_Wf1, L0_gnn_bf1, L0_gnn_Wf2, L0_gnn_bf2, L0_gnn_Wo1, L0_gnn_bo1, L0_gnn_Wo2, L0_gnn_bo2):
    import jax
    import jax.numpy as jnp

    def _L0_gnn_ref(x, rbf, dist_cut, idx_i, idx_j, W_in2f, Wf1, bf1, Wf2, bf2, Wo1, bo1, Wo2, bo2):
        import jax, jax.numpy as jnp
        import numpy as np
        LOG2 = float(np.log(2.0))

        def ssp(x):
            return jax.nn.softplus(x) - LOG2
        N_ATOMS, N_EDGES, N_HF, N_RBF = (25000, 6250, 256, 64)
        n_atoms = x.shape[0]
        h = x @ W_in2f
        Wij = ssp(rbf @ Wf1 + bf1) @ Wf2 + bf2
        Wij = Wij * dist_cut
        x_ij = h[idx_j] * Wij
        m = jax.ops.segment_sum(x_ij, idx_i, num_segments=n_atoms)
        m = ssp(m @ Wo1 + bo1) @ Wo2 + bo2
        return x + m
    h = jnp.maximum(_layernorm(x, axis=-1), 0.0)
    x = x + _L0_gnn_ref(h, edge_attr_64, edge_weight1, src, dst, L0_gnn_W_in2f, L0_gnn_Wf1, L0_gnn_bf1, L0_gnn_Wf2, L0_gnn_bf2, L0_gnn_Wo1, L0_gnn_bo1, L0_gnn_Wo2, L0_gnn_bo2)
    return x

_drawn_inputs = setup_inputs


def setup_inputs(seed=0):
    import zlib

    import numpy as np

    out = dict(_drawn_inputs(seed))
    spreads = {'L0_gnn_bf1': (0.0, 0.8),
     'L0_gnn_bf2': (0.0, 0.8),
     'L0_gnn_bo1': (0.0, 0.268),
     'L0_gnn_bo2': (0.0, 0.1)}
    factors = {'edge_weight1': 3.077}
    for name, (base, spread) in spreads.items():
        noise = np.random.default_rng([zlib.crc32(name.encode()), seed]).standard_normal(out[name].shape)
        drawn = base * np.exp(spread * noise) if base else spread * noise
        out[name] = jnp.asarray(drawn.astype(out[name].dtype))
    for name, factor in factors.items():
        out[name] = (out[name] * factor).astype(out[name].dtype)
    return out
```

```python
import math
from contextlib import ExitStack

import concourse.bass as bass
from concourse import mybir

P = 128
ATOMS, EDGES, F, R = 100000, 25000, 256, 64
KC = F // P
JT = 4
QE = JT * P
QUADS = -(-EDGES // QE)
TILES = QUADS * JT
PAD_EDGES = QUADS * QE
GA = 8
GR = GA * P
GROUPS = -(-ATOMS // GR)
OVERLAP = GROUPS * GR - ATOMS
RING = 24
TABLE_TRASH = -(-(ATOMS + 1) // P) * P
TABLE_ROWS = TABLE_TRASH + P
SUM_ZERO_QUADS = 26
SUM_ROWS = SUM_ZERO_QUADS * GR
SUM_TRASH = PAD_EDGES
OUT_TRASH = TABLE_TRASH
OUT_ROWS = OUT_TRASH + 2 * JT * P
LOG2 = math.log(2.0)
EPS = 1e-5
EXP_CAP = 2.0 ** 60
assert GROUPS == 2 * QUADS and SUM_ROWS >= SUM_TRASH + P
FIRST_LOOK_QUAD = TILES // 8


def build(nc, x, src_cols, src_rows, dst_cols, attr_t, weight_cols, w_in, wf1, bf1, wf2, bf2, wo1, bo1, wo2, bo2, out):
    f32, i32 = mybir.dt.float32, mybir.dt.int32
    ALU, ACT = mybir.AluOpType, mybir.ActivationFunctionType
    ctx = ExitStack()
    with ctx:
        def sb(name, shape, dt=f32):
            return ctx.enter_context(nc.sbuf_tensor(name, shape, dt))

        def ps(name):
            return ctx.enter_context(nc.psum_tensor(name, [P, KC, QE], f32))

        def sem(name):
            return ctx.enter_context(nc.semaphore(name))

        def sems(name, n):
            return [sem(f"{name}{i}") for i in range(n)]

        table = nc.dram_tensor("rep_table", (TABLE_ROWS, 1), i32, kind="Internal").ap()
        sums = nc.dram_tensor("segment_sums", (SUM_ROWS, F), f32, kind="Internal").ap()

        xs = sb("xs", [P, 4, GA, F])
        hs = sb("hs", [P, 2, GA, F])
        ring = sb("ring", [P, RING, JT, F])
        row_now = sb("row_now", [P, 2, JT, F])
        xg = sb("xg", [P, 2, JT, F])
        attr = sb("attr", [R, 2, QE])
        src_row = sb("src_row", [P, 2, QE], i32)
        h_t = sb("h_t", [P, KC, QE])
        soft = sb("soft", [P, KC, QE])
        msg = sb("msg", [P, KC, QE])
        y_rows = sb("y_rows", [P, JT, F])
        same = sb("same", [P, JT, P])
        w_in_s = sb("w_in_s", [P, KC, F])
        wf1_s = sb("wf1_s", [R, F])
        wf2_s = sb("wf2_s", [P, KC, F])
        wo1_s = sb("wo1_s", [P, KC, F])
        wo2_s = sb("wo2_s", [P, KC, F])
        bf1_c = sb("bf1_c", [P, KC])
        bf2_c = sb("bf2_c", [P, KC])
        bo1_c = sb("bo1_c", [P, KC])
        filt_bias = sb("filt_bias", [P, KC])
        sp0 = sb("sp0", [P, KC])
        sp0_shift = sb("sp0_shift", [P, KC])
        lean_row = sb("lean_row", [P, F])
        lone_row = sb("lone_row", [P, F])
        bo2_row = y_rows[:, 2]
        ident = sb("ident", [P, P])
        below = sb("below", [P, P])
        ones = y_rows[:, 3, 0:P]
        zeros = sb("zeros", [P, F])
        neg_log2 = sb("neg_log2", [P, 1])
        warm = sb("warm", [P, 1])
        spare_entry = sb("spare_entry", [P, 2])
        src_i = sb("src_i", [P, TILES], i32)
        dst_i = sb("dst_i", [P, TILES], i32)
        src_f = sb("src_f", [P, TILES])
        weight = sb("weight", [P, TILES])
        edge_i = sb("edge_i", [P, TILES], i32)
        trash_i = sb("trash_i", [P, JT * 2], i32)
        msg_flat = msg[:, :, :].rearrange("p k e -> p (k e)")
        cover, idx_a, idx_b = (msg_flat[:, n * TILES:(n + 1) * TILES] for n in range(3))
        table_idx = sb("table_idx", [P, TILES + JT], i32)
        table_val = sb("table_val", [P, TILES + JT], i32)
        rep_i = sb("rep_i", [P, TILES], i32)
        out_idx = table_val[:, 0:TILES]
        dst_now = sb("dst_now", [P, 2, JT], i32)
        idx_now = sb("idx_now", [P, 2, 8], i32)
        val_now = sb("val_now", [P, 2, 8], i32)
        rep_now = sb("rep_now", [P, 2, 8], i32)
        NS = 2 * GA + JT
        stats = sb("stats", [P, 2, NS, 6])
        st_a = sb("st_a", [P, NS])
        st_b = sb("st_b", [P, NS])
        st_c = sb("st_c", [P, NS])
        st_sum = sb("st_sum", [P, NS])
        st_var = sb("st_var", [P, NS])
        st_ln = sb("st_ln", [P, NS])
        st_seed = sb("st_seed", [P, NS])
        rstd = sb("rstd", [P, 2, NS])
        shift = sb("shift", [P, 2, NS])

        ps_f = ps("ps_f")
        ps_h = ps("ps_h")
        ps_p = ps("ps_p")
        ps_w = ps("ps_w")

        weights_in = sems("weights_in", 15)
        x_loaded = sems("x_loaded", 4)
        out_stored = sems("out_stored", 2)
        attr_loaded = sems("attr_loaded", 2)
        row_loaded = sems("row_loaded", 2)
        pre_loaded = sems("pre_loaded", 2)
        pre_used = sem("pre_used")
        sums_zeroed = sem("sums_zeroed")
        trash_zeroed = sem("trash_zeroed")
        const_made = sem("const_made")
        zero_made = sem("zero_made")
        iota_made = sem("iota_made")
        ident_step = sem("ident_step")
        src_f_made = sem("src_f_made")
        index_step = sem("index_step")
        index_made = sem("index_made")
        setup_dve = sem("setup_dve")
        setup_act = sem("setup_act")
        setup_pe = sem("setup_pe")
        setup_done = sem("setup_done")
        table_written = sem("table_written")
        looked_first = sem("looked_first")
        looked = sems("looked", 2)
        gathered = sems("gathered", 2)
        pool_waits = sem("pool_waits")
        staged = sem("staged")
        rep_saved = sem("rep_saved")
        rows_staged = sem("rows_staged")
        added = sem("added")
        stats_made = sem("stats_made")
        small_step = sem("small_step")
        var_ready = sem("var_ready")
        ln_var = sem("ln_var")
        seed_ready = sem("seed_ready")
        norm_ready = sem("norm_ready")
        edges_normed = sem("edges_normed")
        stream_normed = sem("stream_normed")
        x_added = sem("x_added")
        group_summed = sem("group_summed")
        filt1_done = sem("filt1_done")
        exp_done = sem("exp_done")
        capped = sem("capped")
        log_done = sem("log_done")
        soft_ready = sem("soft_ready")
        transposed = sem("transposed")
        h_t_ready = sem("h_t_ready")
        proj_done = sem("proj_done")
        proj_ready = sem("proj_ready")
        filt2_done = sem("filt2_done")
        msg_ready = sem("msg_ready")
        y_done = sem("y_done")
        y_ready = sem("y_ready")
        same_ready = sem("same_ready")
        merged = sem("merged")
        rows_ready = sem("rows_ready")
        sum_loaded = sems("sum_loaded", 2)
        f_transposed = sem("f_transposed")
        f_exp = sem("f_exp")
        f_capped = sem("f_capped")
        f_log = sem("f_log")
        f_soft = sem("f_soft")
        f_out = sem("f_out")
        f_rows = sem("f_rows")
        out_idx_step = sem("out_idx_step")
        out_idx_made = sem("out_idx_made")
        out_added = sems("out_added", 2)

        block = ctx.enter_context(nc.Block())

        def flat(t):
            return t.rearrange("p a b -> p (a b)")

        def group_rows(dram, base):
            return dram[bass.ds(base, GR), :].rearrange("(p a) f -> p a f", a=GA)

        def group_base(g):
            return 0 if isinstance(g, int) and g == 0 else g * GR - OVERLAP

        def quads(engine, body, split=RING // 2):
            body(0, 0)
            body(1, 1)
            with engine.Fori(1, split) as r:
                body(r * 2, 0)
                body(r * 2 + 1, 1)
            with engine.Fori(split, 23) as r:
                body(r * 2, 0)
                body(r * 2 + 1, 1)
            body(46, 0)
            body(47, 1)
            body(48, 0)

        @block.sync
        def _(sp):
            setup = [(src_i[:, :], src_cols), (dst_i[:, :], dst_cols), (weight[:, :], weight_cols),
                     (wf1_s[:, :], wf1), (w_in_s[:, :, :], w_in.rearrange("(k p) f -> p k f", p=P)),
                     (wf2_s[:, :, :], wf2.rearrange("(k p) f -> p k f", p=P)),
                     (wo1_s[:, :, :], wo1.rearrange("(k p) f -> p k f", p=P)),
                     (wo2_s[:, :, :], wo2.rearrange("(k p) f -> p k f", p=P)),
                     (bf1_c[:, :], bf1), (bf2_c[:, :], bf2), (bo1_c[:, :], bo1),
                     (bo2_row[:, :], bo2.partition_broadcast(P))]
            for n, (dst, s) in enumerate(setup):
                sp.dma_start(dst, s).then_inc(weights_in[n], 16)
            for g in range(4):
                sp.dma_start(xs[:, g], group_rows(x, group_base(g))).then_inc(x_loaded[g], 16)
            for q in range(2):
                sp.dma_start(attr[:, q], attr_t[:, bass.ts(q, QE)]).then_inc(attr_loaded[q], 16)

            def pre_row(q, s, wait=True):
                if wait:
                    sp.wait_ge(pre_used, q - 1)
                sp.dma_start(src_row[:, s], src_rows[bass.ds(q, 1), :].partition_broadcast(P)).then_inc(pre_loaded[s], 16)

            pre_row(0, 0, False)
            pre_row(1, 1, False)
            with sp.Fori(1, QUADS // 2) as r:
                pre_row(r * 2, 0)
                pre_row(r * 2 + 1, 1)
            pre_row(QUADS - 1, 0)
            for q in range(2):
                sp.wait_ge(pre_used, QUADS - 1 + (q == 0))
                sp.dma_start(src_row[:, q], src_rows[q:q + 1, :].partition_broadcast(P)).then_inc(row_loaded[q], 16)
            sp.wait_ge(zero_made, 1)
            sp.dma_start(out[ATOMS:OUT_ROWS, :].rearrange("(p a) f -> p a f", a=(OUT_ROWS - ATOMS) // 112),
                         zeros[0:112, :].unsqueeze(1).broadcast_to([112, (OUT_ROWS - ATOMS) // 112, F])
                         ).then_inc(trash_zeroed, 16)

            def body(q, s, zero=False):
                static = isinstance(q, int)
                if zero:
                    sp.dma_start(group_rows(sums, q * GR), zeros[:, :].unsqueeze(1).broadcast_to([P, GA, F])
                                 ).then_inc(sums_zeroed, 16)
                for h in range(2):
                    sp.wait_ge(group_summed, q * 2 + h + 1)
                    if static and q == 0 and h == 1:
                        sp.wait_ge(out_stored[0], 16)
                    sp.dma_start(group_rows(out, group_base(q * 2 + h)), hs[:, h]).then_inc(out_stored[h], 16)
                    if not static or q < QUADS - 2:
                        sp.dma_start(xs[:, 2 * s + h], group_rows(x, group_base(q * 2 + h + 4))
                                     ).then_inc(x_loaded[2 * s + h], 16)
                if not static or q < QUADS - 2:
                    sp.wait_ge(filt1_done, q + 1)
                    sp.dma_start(attr[:, s], attr_t[:, bass.ds((q + 2) * QE, QE)]).then_inc(attr_loaded[s], 16)
                    sp.wait_ge(same_ready, q + 1)
                    sp.dma_start(src_row[:, s], src_rows[bass.ds(q + 2, 1), :].partition_broadcast(P)
                                 ).then_inc(row_loaded[s], 16)

            body(0, 0, True)
            body(1, 1, True)
            with sp.Fori(1, SUM_ZERO_QUADS // 2) as r:
                body(r * 2, 0, True)
                body(r * 2 + 1, 1, True)
            with sp.Fori(SUM_ZERO_QUADS // 2, 23) as r:
                body(r * 2, 0)
                body(r * 2 + 1, 1)
            body(46, 0)
            body(47, 1)
            body(48, 0)

            sp.wait_ge(added, 16 * TILES)

            def load_sums(q, s, wait=True):
                if wait:
                    sp.wait_ge(f_transposed, q - 1)
                sp.dma_start(ring[:, s], sums[bass.ds(q * QE, QE), :].rearrange("(p j) f -> p j f", j=JT)
                             ).then_inc(sum_loaded[s], 16)

            load_sums(0, 0, False)
            load_sums(1, 1, False)
            with sp.Fori(1, QUADS // 2) as r:
                load_sums(r * 2, 0)
                load_sums(r * 2 + 1, 1)
            load_sums(QUADS - 1, 0)

        @block.gpsimd
        def _(pool):
            pool.memset(ident[:, :], 0.0).then_inc(ident_step, 1)
            pool.memset(ones[:, :], 1.0).then_inc(ident_step, 1)
            pool.iota(edge_i[:, :], [[QE, QUADS], [1, JT]], base=0, channel_multiplier=JT).then_inc(iota_made, 1)
            pool.iota(trash_i[:, :], [[P, 2 * JT]], base=OUT_TRASH, channel_multiplier=1).then_inc(iota_made, 1)
            pool.wait_ge(ident_step, 2)
            pool.affine_select(out=ident[:, :], in_=ident[:, :], compare_op=ALU.not_equal, fill=1.0, base=0,
                               pattern=[[-1, P]], channel_multiplier=1).then_inc(const_made, 1)
            pool.affine_select(out=below[:, :], in_=ones[:, :], compare_op=ALU.is_gt, fill=0.0, base=0,
                               pattern=[[-1, P]], channel_multiplier=1).then_inc(const_made, 1)

            def at(idx):
                return bass.IndirectOffsetOnAxis(ap=idx, axis=0)

            def wait_alone(sem, value):
                pool.wait_ge(sem, value)
                pool.sem_inc(pool_waits, 1)

            def gather(idx, s, j):
                pool.indirect_dma_start(xg[:, s, j], None, x[:, :], at(idx)).then_inc(gathered[s], 16)

            def write_table(t, idx, val):
                if not (isinstance(t, int) and t == 0):
                    wait_alone(table_written, t * 16)
                pool.indirect_dma_start(table[:, :], at(idx), val, None).then_inc(table_written, 16)

            def look(out_rep, idx, done):
                pool.indirect_dma_start(out_rep, None, table[:, :], at(idx)).then_inc(done, 16)

            def add_rows(t, rep, odd, j):
                if not (isinstance(t, int) and t == 0):
                    wait_alone(added, t * 16)
                pool.indirect_dma_start(sums[:, :], at(rep), row_now[:, odd, j], None,
                                        compute_op=ALU.add).then_inc(added, 16)

            pool.wait_ge(weights_in[1], 16)
            for q in range(2):
                for j in range(JT):
                    gather(dst_i[:, q * JT + j:q * JT + j + 1], q, j)

            def early(q, s):
                wait_alone(staged, q + 1)
                for j in range(JT):
                    write_table(q * 8 + 2 * j, idx_now[:, s, 2 * j:2 * j + 1], val_now[:, s, 2 * j:2 * j + 1])
                    if j == 0:
                        wait_alone(transposed, q + 1)
                    gather(dst_now[:, s, j:j + 1], s, j)
                    write_table(q * 8 + 2 * j + 1, idx_now[:, s, 2 * j + 1:2 * j + 2], val_now[:, s, 2 * j + 1:2 * j + 2])

            early(0, 0)
            early(1, 1)
            with pool.Fori(1, FIRST_LOOK_QUAD // 2) as r:
                early(r * 2, 0)
                early(r * 2 + 1, 1)

            for t in range(8 * FIRST_LOOK_QUAD, TILES):
                write_table(t, table_idx[:, t:t + 1], table_val[:, t:t + 1])
            pool.wait_ge(staged, FIRST_LOOK_QUAD + 1)
            pool.wait_ge(transposed, FIRST_LOOK_QUAD + 1)
            for j in range(JT):
                gather(dst_now[:, 0, j:j + 1], 0, j)
            pool.wait_ge(table_written, 16 * TILES)
            for t in range(JT):
                look(rep_i[:, t:t + 1], table_idx[:, t:t + 1], looked_first)
            for i in range(8):
                look(rep_now[:, 0, i:i + 1], table_idx[:, JT + i:JT + i + 1], looked[0])
            pool.wait_ge(sums_zeroed, 16 * SUM_ZERO_QUADS)
            pool.wait_ge(looked_first, 16 * JT)
            pool.wait_ge(rows_staged, 1)
            for t in range(JT):
                add_rows(t, rep_i[:, t:t + 1], 0, t)

            def late(q, s, b_half, last=False, fetch=True):
                par = 1 - s
                first = (q - 25) * 8 + JT
                wait_alone(looked[par], b_half * 128 + 128)
                if not last:
                    wait_alone(staged, q + 1)
                for i in range(8):
                    if i % JT == 0:
                        wait_alone(rows_staged, (q - 25) * 2 + 2 + i // JT)
                    add_rows(first + i, rep_now[:, par, i:i + 1], 1 - i // JT, i % JT)
                    if not last:
                        if i == 0 and not (isinstance(q, int) and q == 25):
                            wait_alone(rep_saved, q - 25)
                        look(rep_now[:, s, i:i + 1], idx_now[:, s, i:i + 1], looked[s])
                    if fetch and i % 2:
                        if i == 1:
                            wait_alone(transposed, q + 1)
                        gather(dst_now[:, s, i // 2:i // 2 + 1], s, i // 2)

            late(25, 1, 0)
            with pool.Fori(13, 23) as r:
                late(r * 2, 0, r - 13)
                late(r * 2 + 1, 1, r - 12)
            late(46, 0, 10)
            late(47, 1, 11, fetch=False)
            late(48, 0, 11, last=True, fetch=False)

            for h in range(2):
                pool.wait_ge(out_stored[h], 16 * QUADS)
            pool.wait_ge(trash_zeroed, 16)

            def add_out(q, s, wait=True):
                wait_alone(f_rows, q + 1)
                if wait:
                    wait_alone(out_added[s], (q - s) * 32)
                for j in range(JT):
                    pool.indirect_dma_start(out[:, :], at(dst_now[:, s, j:j + 1]), ring[:, 4 + s, j], None,
                                            compute_op=ALU.add).then_inc(out_added[s], 16)

            add_out(0, 0, False)
            add_out(1, 1, False)
            with pool.Fori(1, QUADS // 2) as r:
                add_out(r * 2, 0)
                add_out(r * 2 + 1, 1)
            add_out(QUADS - 1, 0)
            pool.wait_ge(out_added[0], 64 * (QUADS // 2 + 1))
            pool.wait_ge(out_added[1], 64 * (QUADS // 2))

        @block.scalar
        def _(act):
            act.wait_ge(setup_dve, 1)
            act.activation(warm[:, :], warm[:, :], ACT.Ln, bias=1.0)
            act.wait_ge(weights_in[10], 16)
            act.activation(sp0[:, :], bo1_c[:, :], ACT.Exp).then_inc(setup_act, 1)
            act.wait_ge(setup_dve, 2)
            act.activation(sp0[:, :], sp0[:, :], ACT.Ln, bias=1.0).then_inc(setup_act, 1)

            def seed(n):
                act.wait_ge(var_ready, n)
                act.activation(st_ln[:, :], st_var[:, :], ACT.Ln).then_inc(ln_var, 1)
                act.wait_ge(ln_var, n)
                act.activation(st_seed[:, :], st_ln[:, :], ACT.Exp, scale=-0.5).then_inc(seed_ready, 1)

            seed(1)

            def body(q, s, slot=None, last=False):
                static = isinstance(q, int)

                def norm_stream(half):
                    h, a0 = half // 2, (half % 2) * 4
                    if half % 2 == 0 and not (static and q == 0):
                        act.wait_ge(out_stored[h], q * 16)
                    for a in range(a0, a0 + 4):
                        c = h * GA + a
                        ins = act.activation(hs[:, h, a], xs[:, 2 * s + h, a], ACT.Relu,
                                             bias=shift[:, s, c:c + 1], scale=rstd[:, s, c:c + 1])
                    ins.then_inc(stream_normed, 1)

                act.wait_ge(norm_ready, q + 1)
                for j in range(JT):
                    c = 2 * GA + j
                    ins = act.activation(xg[:, s, j], xg[:, s, j], ACT.Relu,
                                         bias=shift[:, s, c:c + 1], scale=rstd[:, s, c:c + 1])
                ins.then_inc(edges_normed, 1)
                act.wait_ge(filt1_done, q + 1)
                if not (static and q == 0):
                    act.wait_ge(filt2_done, q)
                for k in range(KC):
                    ins = act.activation(soft[:, k], ps_f[:, k], ACT.Exp, bias=bf1_c[:, k:k + 1])
                ins.then_inc(exp_done, 1)
                norm_stream(0)
                act.wait_ge(transposed, q + 1)
                if not (static and q == 0):
                    act.wait_ge(proj_done, q)
                for k in range(KC):
                    ins = act.activation(h_t[:, k], ps_h[:, k], ACT.Copy)
                ins.then_inc(h_t_ready, 1)
                act.wait_ge(capped, q + 1)
                act.activation(flat(soft[:, :, :]), flat(soft[:, :, :]), ACT.Ln, bias=1.0).then_inc(log_done, 1)
                norm_stream(1)
                act.wait_ge(proj_done, q + 1)
                if not (static and q == 0):
                    act.wait_ge(y_done, q)
                for k in range(KC):
                    ins = act.activation(msg[:, k], ps_p[:, k], ACT.Copy)
                ins.then_inc(proj_ready, 1)
                norm_stream(2)
                act.wait_ge(y_done, q + 1)
                if not (static and q == 0):
                    act.wait_ge(merged, q)
                y_flat = flat(y_rows[:, :, :])
                for k in range(KC):
                    ins = act.activation(y_flat[:, bass.ts(k, QE)], ps_f[:, k], ACT.Copy)
                ins.then_inc(y_ready, 1)
                norm_stream(3)
                if not last:
                    seed(q + 2)
                act.wait_ge(merged, q + 1)
                if slot is None:
                    slot = q
                else:
                    act.wait_ge(rows_staged, q - RING + 1)
                dst = ring[:, bass.ds(slot, 1)].rearrange("p o j f -> p (o j f)")
                for k in range(KC):
                    ins = act.activation(dst[:, bass.ts(k, QE)], ps_h[:, k], ACT.Copy)
                ins.then_inc(rows_ready, 1)

            body(0, 0)
            body(1, 1)
            with act.Fori(1, RING // 2) as r:
                body(r * 2, 0)
                body(r * 2 + 1, 1)
            with act.Fori(RING // 2, 23) as r:
                body(r * 2, 0, r * 2 - RING)
                body(r * 2 + 1, 1, r * 2 + 1 - RING)
            body(46, 0, 46 - RING)
            body(47, 1, 47 - RING)
            body(48, 0, 0, last=True)

            def f_first(q, s, wait=True):
                act.wait_ge(f_transposed, q + 1)
                if wait:
                    act.wait_ge(f_out, q - 1)
                for k in range(KC):
                    pst = (ps_f, ps_h)[s]
                    ins = act.activation(flat(ring[:, 2 + s])[:, bass.ts(k, QE)], pst[:, k], ACT.Exp,
                                         bias=bo1_c[:, k:k + 1])
                ins.then_inc(f_exp, 1)

            def f_second(q, s):
                act.wait_ge(f_capped, q + 1)
                act.activation(flat(ring[:, 2 + s]), flat(ring[:, 2 + s]), ACT.Ln, bias=1.0).then_inc(f_log, 1)

            f_first(0, 0, False)
            f_first(1, 1, False)
            f_second(0, 0)
            with act.Fori(1, QUADS // 2) as r:
                f_first(r * 2, 0)
                f_second(r * 2 - 1, 1)
                f_first(r * 2 + 1, 1)
                f_second(r * 2, 0)
            f_first(QUADS - 1, 0)
            f_second(QUADS - 2, 1)
            f_second(QUADS - 1, 0)

        @block.tensor
        def _(pe):
            pe.wait_ge(const_made, 1)
            for n in range(3, 8):
                pe.wait_ge(weights_in[n], 16)
            pe.wait_ge(setup_dve, 1)
            for c in range(KC):
                for k in range(KC):
                    ins = pe.matmul(ps_w[:, 0, c:c + 1], wf2_s[:, k, bass.ts(c, P)], neg_log2[:, :],
                                    start=(k == 0), stop=(k == KC - 1))
            ins.then_inc(setup_pe, 1)
            pe.wait_ge(setup_dve, 6)
            for v in range(2):
                for k in range(KC):
                    ins = pe.matmul(ps_p[:, v, 0:F], y_rows[:, k, v * P:(v + 1) * P], wo2_s[:, k],
                                    start=(k == 0), stop=(k == KC - 1))
            ins.then_inc(setup_pe, 1)
            pe.wait_ge(setup_done, 1)

            def body(q, s):
                static = isinstance(q, int)
                pe.wait_ge(attr_loaded[s], q * 8 + (16 if s == 0 else 8))
                if not (static and q == 0):
                    pe.wait_ge(y_ready, q)
                for c in range(KC):
                    ins = pe.matmul(ps_f[:, c], wf1_s[:, bass.ts(c, P)], attr[:, s], start=True, stop=True)
                ins.then_inc(filt1_done, 1)
                pe.wait_ge(edges_normed, q + 1)
                if not (static and q == 0):
                    pe.wait_ge(rows_ready, q)
                for k in range(KC):
                    for j in range(JT):
                        ins = pe.transpose(ps_h[:, k, bass.ts(j, P)], xg[:, s, j, bass.ts(k, P)], ident[:, :])
                ins.then_inc(transposed, 1)
                pe.wait_ge(h_t_ready, q + 1)
                if not (static and q == 0):
                    pe.wait_ge(proj_ready, q)
                for c in range(KC):
                    for k in range(KC):
                        ins = pe.matmul(ps_p[:, c], w_in_s[:, k, bass.ts(c, P)], h_t[:, k],
                                        start=(k == 0), stop=(k == KC - 1))
                ins.then_inc(proj_done, 1)
                pe.wait_ge(soft_ready, q + 1)
                if not (static and q == 0):
                    pe.wait_ge(msg_ready, q)
                for c in range(KC):
                    for k in range(KC):
                        ins = pe.matmul(ps_w[:, c], wf2_s[:, k, bass.ts(c, P)], soft[:, k],
                                        start=(k == 0), stop=(k == KC - 1))
                ins.then_inc(filt2_done, 1)
                pe.wait_ge(msg_ready, q + 1)
                rows = ps_f[:, :, :].rearrange("p k (a f) -> p (k a) f", f=F)
                for j in range(JT):
                    for k in range(KC):
                        ins = pe.matmul(rows[:, j], msg[:, k, bass.ts(j, P)], wo1_s[:, k],
                                        start=(k == 0), stop=(k == KC - 1))
                ins.then_inc(y_done, 1)
                pe.wait_ge(y_ready, q + 1)
                pe.wait_ge(same_ready, q + 1)
                rows = ps_h[:, :, :].rearrange("p k (a f) -> p (k a) f", f=F)
                for j in range(JT):
                    ins = pe.matmul(rows[:, j], same[:, j], y_rows[:, j], start=True, stop=True)
                ins.then_inc(merged, 1)

            quads(pe, body)

            def f_turn(q, s, wait=True):
                pe.wait_ge(sum_loaded[s], q * 8 + (16 if s == 0 else 8))
                if wait:
                    pe.wait_ge(f_soft, q - 1)
                for k in range(KC):
                    for j in range(JT):
                        ins = pe.transpose((ps_f, ps_h)[s][:, k, bass.ts(j, P)], ring[:, s, j, bass.ts(k, P)], ident[:, :])
                ins.then_inc(f_transposed, 1)

            def f_mul(q, s, wait=True):
                pe.wait_ge(f_soft, q + 1)
                if wait:
                    pe.wait_ge(f_rows, q - 1)
                sp_t = flat(ring[:, 2 + s]).rearrange("p (k e) -> p k e", k=KC)
                rows = (ps_p, ps_w)[s][:, :, :].rearrange("p k (a f) -> p (k a) f", f=F)
                for j in range(JT):
                    for k in range(KC):
                        ins = pe.matmul(rows[:, j], sp_t[:, k, bass.ts(j, P)], wo2_s[:, k],
                                        start=(k == 0), stop=(k == KC - 1))
                ins.then_inc(f_out, 1)

            pe.wait_ge(rows_ready, QUADS)
            f_turn(0, 0, False)
            f_turn(1, 1, False)
            f_mul(0, 0, False)
            with pe.Fori(1, QUADS // 2) as r:
                f_turn(r * 2, 0)
                f_mul(r * 2 - 1, 1)
                f_turn(r * 2 + 1, 1)
                f_mul(r * 2, 0)
            f_turn(QUADS - 1, 0)
            f_mul(QUADS - 2, 1)
            f_mul(QUADS - 1, 0)

        @block.vector
        def _(dve):
            dve.memset(neg_log2[:, :], -LOG2)
            dve.memset(warm[:, :], 1.0).then_inc(setup_dve, 1)
            dve.memset(zeros[:, :], 0.0).then_inc(zero_made, 1)

            dve.wait_ge(weights_in[0], 16)
            dve.tensor_copy(src_f[:, :], src_i[:, :]).then_inc(src_f_made, 1)
            dve.wait_ge(src_f_made, 1)
            dve.wait_ge(const_made, 2)

            def pre(q, s, wait=True):
                if wait:
                    dve.wait_ge(pre_used, q)
                dve.wait_ge(pre_loaded[s], q * 8 + (16 if s == 0 else 8))
                for j in range(JT):
                    ins = dve.scalar_tensor_tensor(out=same[:, j], in0=src_row[:, s, bass.ts(j, P)],
                                                   scalar=src_f[:, bass.ds(q * JT + j, 1)], in1=below[:, :],
                                                   op0=ALU.is_equal, op1=ALU.mult,
                                                   accum_out=cover[:, bass.ds(q * JT + j, 1)])
                ins.then_inc(pre_used, 1)

            pre(0, 0, False)
            pre(1, 1)
            with dve.Fori(1, QUADS // 2) as r:
                pre(r * 2, 0)
                pre(r * 2 + 1, 1)
            pre(QUADS - 1, 0)

            steps = [0]

            def step(ins):
                ins.then_inc(index_step, 1)
                steps[0] += 1
                dve.wait_ge(index_step, steps[0])

            dve.wait_ge(pre_used, QUADS)
            dve.wait_ge(iota_made, 2)
            step(dve.tensor_scalar(cover[:, :], cover[:, :], 1.0, None, ALU.min))
            step(dve.tensor_scalar(spare_entry[:, 0:1], trash_i[:, 0:1], float(TABLE_TRASH - OUT_TRASH), None, ALU.add))
            step(dve.tensor_scalar(idx_a[:, :], src_f[:, :], spare_entry[:, 0:1], -1.0, ALU.subtract, ALU.mult))
            step(dve.tensor_tensor(idx_a[:, :], idx_a[:, :], cover[:, :], ALU.mult))
            dve.memset(table_idx[:, TILES:], 0)
            dve.memset(table_val[:, TILES:], 0)
            dve.tensor_tensor(table_idx[:, 0:TILES], idx_a[:, :], src_f[:, :], ALU.add)
            step(dve.tensor_scalar(spare_entry[:, 1:2], spare_entry[:, 0:1], float(SUM_TRASH - TABLE_TRASH), None, ALU.add))
            step(dve.tensor_scalar(idx_b[:, :], edge_i[:, :], spare_entry[:, 1:2], -1.0, ALU.subtract, ALU.mult))
            step(dve.tensor_tensor(idx_b[:, :], idx_b[:, :], cover[:, :], ALU.mult))
            dve.tensor_tensor(table_val[:, 0:TILES], idx_b[:, :], edge_i[:, :], ALU.add).then_inc(index_made, 1)

            def stage(n, s, late):
                if isinstance(n, int) and n >= QUADS - 2:
                    pass
                else:
                    dve.tensor_copy(dst_now[:, s], dst_i[:, bass.ds((n + 2) * JT, JT)])
                if late:
                    ins = dve.tensor_copy(idx_now[:, s], table_idx[:, bass.ds((n - 25) * 8 + 3 * JT, 8)])
                else:
                    dve.tensor_copy(idx_now[:, s], table_idx[:, bass.ds(n * 8, 8)])
                    ins = dve.tensor_copy(val_now[:, s], table_val[:, bass.ds(n * 8, 8)])
                ins.then_inc(staged, 1)

            dve.wait_ge(index_made, 1)
            dve.wait_ge(weights_in[1], 16)
            stage(0, 0, False)

            dve.wait_ge(setup_act, 1)
            dve.tensor_scalar(sp0[:, :], sp0[:, :], EXP_CAP, None, ALU.min).then_inc(setup_dve, 1)
            dve.wait_ge(setup_act, 2)
            dve.tensor_tensor(sp0[:, :], sp0[:, :], bo1_c[:, :], ALU.max).then_inc(setup_dve, 1)
            dve.wait_ge(setup_dve, 3)
            dve.tensor_scalar(sp0_shift[:, :], sp0[:, :], -LOG2, None, ALU.add).then_inc(setup_dve, 1)
            dve.wait_ge(setup_dve, 4)
            for v, s0 in enumerate((sp0, sp0_shift)):
                for k in range(KC):
                    ins = dve.tensor_scalar(y_rows[:, k, v * P:(v + 1) * P], ones[:, :], s0[:, k:k + 1], None, ALU.mult)
                ins.then_inc(setup_dve, 1)
            dve.wait_ge(setup_pe, 1)
            dve.wait_ge(weights_in[9], 16)
            dve.tensor_tensor(filt_bias[:, :], ps_w[:, 0, 0:KC], bf2_c[:, :], ALU.add)
            dve.wait_ge(setup_pe, 2)
            dve.wait_ge(weights_in[11], 16)
            dve.tensor_copy(lean_row[:, :], ps_p[:, 0, 0:F])
            dve.tensor_tensor(lone_row[:, :], ps_p[:, 1, 0:F], bo2_row[:, :], ALU.add).then_inc(setup_done, 1)
            dve.wait_ge(setup_done, 1)
            for n in (2, 8):
                dve.wait_ge(weights_in[n], 16)

            def stream_stats(q, s, h):
                dve.wait_ge(x_loaded[2 * s + h], q * 8 + (16 if s == 0 else 8))
                for a in range(GA):
                    ins = dve.bn_stats(stats[:, s, h * GA + a], xs[:, 2 * s + h, a])
                if h == 1:
                    ins.then_inc(stats_made, 1)

            def edge_stats(q, s):
                dve.wait_ge(gathered[s], q * 32 + (64 if s == 0 else 32))
                for j in range(JT):
                    dve.bn_stats(stats[:, s, 2 * GA + j], xg[:, s, j])

            def variance(q, s):
                def wait(n):
                    dve.wait_ge(small_step, q * 8 + n)
                dve.wait_ge(stats_made, q + 1)
                me, mo = stats[:, s, :, 1], stats[:, s, :, 4]
                dve.tensor_tensor(st_a[:, :], me, mo, ALU.subtract).then_inc(small_step, 1)
                dve.tensor_tensor(st_b[:, :], stats[:, s, :, 2], stats[:, s, :, 5], ALU.add).then_inc(small_step, 1)
                dve.tensor_tensor(st_sum[:, :], me, mo, ALU.add)
                wait(1)
                dve.scalar_tensor_tensor(out=st_c[:, :], in0=st_a[:, :], scalar=0.25, in1=st_a[:, :],
                                         op0=ALU.mult, op1=ALU.mult).then_inc(small_step, 1)
                wait(3)
                dve.scalar_tensor_tensor(out=st_a[:, :], in0=st_b[:, :], scalar=1.0 / F, in1=st_c[:, :],
                                         op0=ALU.mult, op1=ALU.add).then_inc(small_step, 1)
                wait(4)
                dve.tensor_scalar(st_var[:, :], st_a[:, :], EPS, None, ALU.add).then_inc(var_ready, 1)

            def norm(q, s):
                def wait(n):
                    dve.wait_ge(small_step, q * 8 + n)
                dve.wait_ge(seed_ready, q + 1)
                dve.tensor_tensor(st_b[:, :], st_seed[:, :], st_seed[:, :], ALU.mult).then_inc(small_step, 1)
                wait(5)
                dve.tensor_tensor(st_c[:, :], st_b[:, :], st_var[:, :], ALU.mult).then_inc(small_step, 1)
                wait(6)
                dve.tensor_scalar(st_a[:, :], st_c[:, :], -0.5, 1.5, ALU.mult, ALU.add).then_inc(small_step, 1)
                wait(7)
                dve.tensor_tensor(rstd[:, s], st_seed[:, :], st_a[:, :], ALU.mult).then_inc(small_step, 1)
                wait(8)
                dve.scalar_tensor_tensor(out=shift[:, s], in0=st_sum[:, :], scalar=-0.5, in1=rstd[:, s],
                                         op0=ALU.mult, op1=ALU.mult).then_inc(norm_ready, 1)

            stream_stats(0, 0, 0)
            edge_stats(0, 0)
            stream_stats(0, 0, 1)
            variance(0, 0)
            norm(0, 0)

            def stage_rows(n, odd, slot, first=False):
                dve.wait_ge(rows_ready, n + 1)
                if not first:
                    dve.wait_ge(added, (n - 1) * (16 * JT))
                dve.tensor_copy(row_now[:, odd], ring[:, bass.ds(slot, 1)].squeeze(1)).then_inc(rows_staged, 1)

            def body(q, s, late=False, keep=False, b_half=None, last=False, wrap=False, last_odd=False):
                static = isinstance(q, int)
                back = RING if wrap else 0

                def combine(h):
                    for b in range(2):
                        dve.wait_ge(stream_normed, q * 4 + 2 * h + b + 1)
                        sl = slice(4 * b, 4 * b + 4)
                        dve.tensor_tensor(hs[:, h, sl], hs[:, h, sl], xs[:, 2 * s + h, sl], ALU.add).then_inc(x_added, 1)
                    for b in range(2):
                        sl = slice(4 * b, 4 * b + 4)
                        dve.wait_ge(x_added, q * 4 + 2 * h + b + 1)
                        ins = dve.tensor_tensor(hs[:, h, sl], hs[:, h, sl],
                                                lone_row[:, :].unsqueeze(1).broadcast_to([P, 4, F]), ALU.add)
                    ins.then_inc(group_summed, 1)

                if keep and not last:
                    stage_rows(q * 2 - 48, 0, q * 2 - 48 - back)
                dve.wait_ge(row_loaded[s], q * 8 + (16 if s == 0 else 8))
                if not (static and q == 0):
                    dve.wait_ge(merged, q)
                for j in range(JT):
                    ins = dve.tensor_scalar(same[:, j], src_row[:, s, bass.ts(j, P)],
                                            src_f[:, bass.ds(q * JT + j, 1)], weight[:, bass.ds(q * JT + j, 1)],
                                            ALU.is_equal, ALU.mult)
                ins.then_inc(same_ready, 1)
                if not last:
                    stream_stats(q + 1, 1 - s, 0)
                dve.wait_ge(exp_done, q + 1)
                dve.tensor_scalar(flat(soft[:, :, :]), flat(soft[:, :, :]), EXP_CAP, None, ALU.min).then_inc(capped, 1)
                if not last:
                    edge_stats(q + 1, 1 - s)
                    if not late:
                        if not (static and q == 0):
                            dve.wait_ge(table_written, q * 128)
                        stage(q + 1, 1 - s, False)
                    elif not (static and q == QUADS - 2):
                        if not (static and q == 24):
                            dve.wait_ge(looked[1 - s], b_half * 128 + 128)
                        else:
                            dve.wait_ge(table_written, 16 * TILES)
                        stage(q + 1, 1 - s, True)
                if keep:
                    dve.wait_ge(looked[1 - s], b_half * 128 + 128)
                    dve.tensor_copy(rep_i[:, bass.ds((q - 25) * 8 + JT, 8)], rep_now[:, 1 - s]).then_inc(rep_saved, 1)
                dve.wait_ge(log_done, q + 1)
                for k in range(KC):
                    ins = dve.scalar_tensor_tensor(out=soft[:, k], in0=ps_f[:, k], scalar=bf1_c[:, k:k + 1],
                                                   in1=soft[:, k], op0=ALU.add, op1=ALU.max)
                ins.then_inc(soft_ready, 1)
                combine(0)
                if keep and not (last or last_odd):
                    stage_rows(q * 2 - 47, 1, q * 2 - 47 - back)
                dve.wait_ge(filt2_done, q + 1)
                dve.wait_ge(proj_ready, q + 1)
                for k in range(KC):
                    ins = dve.scalar_tensor_tensor(out=msg[:, k], in0=ps_w[:, k], scalar=filt_bias[:, k:k + 1],
                                                   in1=msg[:, k], op0=ALU.add, op1=ALU.mult)
                ins.then_inc(msg_ready, 1)
                if not last:
                    stream_stats(q + 1, 1 - s, 1)
                    variance(q + 1, 1 - s)
                combine(1)
                if not last:
                    norm(q + 1, 1 - s)

            body(0, 0)
            stage_rows(0, 0, 0, first=True)
            body(1, 1)
            with dve.Fori(1, FIRST_LOOK_QUAD // 2) as r:
                body(r * 2, 0)
                body(r * 2 + 1, 1)
            body(24, 0, late=True)
            stage_rows(1, 1, 1, first=True)
            body(25, 1, late=True, keep=True, b_half=0)
            with dve.Fori(13, 18) as r:
                body(r * 2, 0, True, True, r - 13)
                body(r * 2 + 1, 1, True, True, r - 12)
            with dve.Fori(18, 23) as r:
                body(r * 2, 0, True, True, r - 13, wrap=True)
                body(r * 2 + 1, 1, True, True, r - 12, wrap=True)
            body(46, 0, True, True, 10, wrap=True)
            body(47, 1, True, True, 11, wrap=True, last_odd=True)
            stage_rows(47, 1, 47 - RING)
            body(48, 0, True, True, 11, last=True)
            stage_rows(48, 0, 0)

            dve.wait_ge(looked_first, 16 * JT)
            dve.wait_ge(looked[0], 128 * 12)
            dve.wait_ge(looked[1], 128 * 12)
            dve.wait_ge(y_done, QUADS)
            def ostep(ins):
                steps.append(0)
                ins.then_inc(out_idx_step, 1)
                dve.wait_ge(out_idx_step, len(steps) - 1)
            def spread():
                return trash_i[:, :].unsqueeze(1).broadcast_to([P, TILES // 8, 8])
            half = TILES // 8 * 8
            def parts(t):
                return ((t[:, 0:half].rearrange("p (a b) -> p a b", b=8), spread()),
                        (t[:, half:TILES], trash_i[:, 0:TILES - half]))
            ostep(dve.tensor_tensor(idx_a[:, :], rep_i[:, :], edge_i[:, :], ALU.is_equal))
            for (o, tr), (i, _) in zip(parts(idx_b), parts(src_f)):
                ins = dve.tensor_tensor(o, i, tr, ALU.subtract)
            ostep(ins)
            ostep(dve.tensor_tensor(idx_b[:, :], idx_b[:, :], idx_a[:, :], ALU.mult))
            for (o, tr), (i, _) in zip(parts(out_idx), parts(idx_b)):
                ins = dve.tensor_tensor(o, i, tr, ALU.add)
            ins.then_inc(out_idx_made, 1)
            dve.wait_ge(out_idx_made, 1)

            def f_cap(q, s):
                dve.wait_ge(f_exp, q + 1)
                e = flat(ring[:, 2 + s])
                dve.tensor_scalar(e, e, EXP_CAP, None, ALU.min).then_inc(f_capped, 1)

            def f_max(q, s):
                dve.wait_ge(f_log, q + 1)
                for k in range(KC):
                    e = flat(ring[:, 2 + s])[:, bass.ts(k, QE)]
                    ins = dve.scalar_tensor_tensor(out=e, in0=(ps_f, ps_h)[s][:, k], scalar=bo1_c[:, k:k + 1],
                                                   in1=e, op0=ALU.add, op1=ALU.max)
                ins.then_inc(f_soft, 1)

            def f_sub(q, s, wait=True):
                dve.wait_ge(f_out, q + 1)
                if wait:
                    dve.wait_ge(out_added[s], (q - s) * 32)
                dve.tensor_copy(dst_now[:, s], out_idx[:, bass.ds(q * JT, JT)])
                rows = (ps_p, ps_w)[s][:, :, :].rearrange("p k (a f) -> p (k a) f", f=F)
                for a in range(2):
                    ins = dve.tensor_tensor(ring[:, 4 + s, 2 * a:2 * a + 2], rows[:, 2 * a:2 * a + 2],
                                            lean_row[:, :].unsqueeze(1).broadcast_to([P, 2, F]), ALU.subtract)
                ins.then_inc(f_rows, 1)

            f_cap(0, 0)
            f_cap(1, 1)
            f_max(0, 0)
            f_sub(0, 0, False)
            f_cap(2, 0)
            f_max(1, 1)
            f_sub(1, 1, False)
            with dve.Fori(1, QUADS // 2) as r:
                f_cap(r * 2 + 1, 1)
                f_max(r * 2, 0)
                f_sub(r * 2, 0)
                f_cap(r * 2 + 2, 0)
                f_max(r * 2 + 1, 1)
                f_sub(r * 2 + 1, 1)
            f_max(QUADS - 1, 0)
            f_sub(QUADS - 1, 0)


def kernel(**inputs):
    import numpy as np
    import concourse.bacc as bacc
    from concourse import mybir as mb
    from concourse.bass_utils import run_bass_kernel_spmd as run

    nc = bacc.Bacc("TRN2", target_bir_lowering=False, num_devices=1)
    a = {k: np.asarray(v) for k, v in inputs.items()}

    def padded(v, fill):
        return np.concatenate([v, np.full((PAD_EDGES - EDGES,) + v.shape[1:], fill, v.dtype)])

    def cols(v, fill):
        return np.ascontiguousarray(padded(v, fill).reshape(QUADS, P, JT).transpose(1, 0, 2).reshape(P, TILES))

    def by_tile(v, fill):
        v = padded(v, fill)
        return v.reshape((QUADS, P, JT) + v.shape[1:]).swapaxes(1, 2).reshape((QUADS, QE) + v.shape[1:])

    def chunked(v):
        return np.ascontiguousarray(v.reshape(KC, P).T)

    arrays = {
        "x": np.ascontiguousarray(a["x"]),
        "src_cols": cols(a["src"], ATOMS),
        "src_rows": np.ascontiguousarray(by_tile(a["src"], ATOMS)),
        "dst_cols": cols(a["dst"], 0),
        "attr_t": np.ascontiguousarray(by_tile(a["edge_attr_64"], 0).reshape(PAD_EDGES, R).T),
        "weight_cols": cols(a["edge_weight1"][:, 0], 0),
        "w_in": a["L0_gnn_W_in2f"], "wf1": a["L0_gnn_Wf1"], "bf1": chunked(a["L0_gnn_bf1"]),
        "wf2": a["L0_gnn_Wf2"], "bf2": chunked(a["L0_gnn_bf2"]), "wo1": a["L0_gnn_Wo1"],
        "bo1": chunked(a["L0_gnn_bo1"]), "wo2": a["L0_gnn_Wo2"], "bo2": a["L0_gnn_bo2"].reshape(1, F),
    }
    feeds = {f"in_{k}": np.ascontiguousarray(v) for k, v in arrays.items()}
    args = [nc.dram_tensor(k, v.shape, mb.dt.from_np(v.dtype), kind="ExternalInput").ap() for k, v in feeds.items()]
    out = nc.dram_tensor("out_rows", (OUT_ROWS, F), mb.dt.float32, kind="ExternalOutput").ap()
    build(nc, *args, out)
    r = run(nc, [feeds], core_ids=[0])
    return r.results[0]["out_rows"][:ATOMS]
```

```python
import math
from contextlib import ExitStack

import concourse.bass as bass
from concourse import mybir

P = 128
ATOMS, EDGES, F, R = 100000, 25000, 256, 64
KC = F // P
JT = 4
QE = JT * P
QUADS = -(-EDGES // QE)
TILES = QUADS * JT
PAD_EDGES = QUADS * QE
GA = 8
GR = GA * P
GROUPS = -(-ATOMS // GR)
OVERLAP = GROUPS * GR - ATOMS
RING = 16
WRITE_QUADS = 3
EARLY = QUADS // WRITE_QUADS
TABLE_TRASH = -(-(ATOMS + 1) // P) * P
TABLE_ROWS = TABLE_TRASH + QE
SUM_TRASH = PAD_EDGES
ZERO_A = 16
ZERO_QUADS = 14
SUM_ROWS = ZERO_QUADS * ZERO_A * P
OUT_TRASH = TABLE_TRASH
OUT_ROWS = OUT_TRASH + 2 * QE
LOG2 = math.log(2.0)
EPS = 1e-5
EXP_CAP = 2.0 ** 60
assert GROUPS == 2 * QUADS and SUM_ROWS >= SUM_TRASH + QE and ZERO_QUADS <= EARLY
assert QUADS == WRITE_QUADS * EARLY + 1 and EARLY % 2 == 0 and QUADS % 2 == 1


def build(nc, x, src_cols, src_rows, dst_cols, attr_t, weight_cols, w_in, wf1, bf1, wf2, bf2, wo1, bo1, wo2, bo2, out):
    f32, i32 = mybir.dt.float32, mybir.dt.int32
    ALU, ACT = mybir.AluOpType, mybir.ActivationFunctionType
    ctx = ExitStack()
    with ctx:
        def sb(name, shape, dt=f32):
            return ctx.enter_context(nc.sbuf_tensor(name, shape, dt))

        def ps(name):
            return ctx.enter_context(nc.psum_tensor(name, [P, KC, QE], f32))

        def sem(name):
            return ctx.enter_context(nc.semaphore(name))

        def sems(name, n):
            return [sem(f"{name}{i}") for i in range(n)]

        table = nc.dram_tensor("rep_table", (TABLE_ROWS, 1), i32, kind="Internal").ap()
        sums = nc.dram_tensor("segment_sums", (SUM_ROWS, F), f32, kind="Internal").ap()

        xs = sb("xs", [P, 4, GA, F])
        hs = sb("hs", [P, 2, GA, F])
        ring = sb("ring", [P, RING, JT, F])
        row_now = sb("row_now", [P, 3, JT, F])
        xg = sb("xg", [P, 2, JT, F])
        attr = sb("attr", [R, 2, QE])
        src_row = sb("src_row", [P, 2, QE], i32)
        h_t = sb("h_t", [P, KC, QE])
        soft = sb("soft", [P, KC, QE])
        msg = sb("msg", [P, KC, QE])
        y_rows = sb("y_rows", [P, JT, F])
        same = sb("same", [P, JT, QE])
        pre_row = sb("pre_row", [P, 3, QE], i32)
        hits = sb("hits", [P, JT * (JT + 1) // 2 * P], mybir.dt.bfloat16)
        w_in_s = sb("w_in_s", [P, KC, F])
        wf1_s = sb("wf1_s", [R, F])
        wf2_s = sb("wf2_s", [P, KC, F])
        wo1_s = sb("wo1_s", [P, KC, F])
        wo2_s = sb("wo2_s", [P, KC, F])
        bf1_c = sb("bf1_c", [P, KC])
        bf2_c = sb("bf2_c", [P, KC])
        bo1_c = sb("bo1_c", [P, KC])
        filt_bias = sb("filt_bias", [P, KC])
        sp0 = sb("sp0", [P, KC])
        sp0_shift = sb("sp0_shift", [P, KC])
        lean_row = sb("lean_row", [P, F])
        lone_row = sb("lone_row", [P, F])
        bo2_row = y_rows[:, 2]
        lone_hi, lone_mid = hits[:, 0:F], hits[:, F:2 * F]
        lone_rest, lone_low = msg[:, 0, 0:F], msg[:, 0, F:2 * F]
        lone_sum = msg[:, 1, 0:F]
        ident = sb("ident", [P, P])
        earlier = sb("earlier", [P, JT, P])
        bf16 = mybir.dt.bfloat16
        all_ones = sb("all_ones", [P, P], bf16)
        lone_parts = sb("lone_parts", [P, 2, F], bf16)
        ones = y_rows[:, 3, 0:P]
        zeros = sb("zeros", [P, F])
        neg_log2 = sb("neg_log2", [P, 1])
        src_i = sb("src_i", [P, TILES], i32)
        dst_i = sb("dst_i", [P, TILES], i32)
        src_f = sb("src_f", [P, TILES])
        weight = sb("weight", [P, TILES])
        edge_i = sb("edge_i", [P, TILES], i32)
        trash_i = sb("trash_i", [P, JT * 2], i32)
        table_idx = sb("table_idx", [P, TILES], i32)
        spare_table = sb("spare_table", [P, TILES], i32)
        spare_less_src = sb("spare_less_src", [P, TILES])
        spare_sum = sb("spare_sum", [P, TILES], i32)
        rep_i = sb("rep_i", [P, TILES], i32)
        out_idx = spare_table
        dst_now = sb("dst_now", [P, 2, JT], i32)
        idx_now = sb("idx_now", [P, 2, WRITE_QUADS * JT], i32)
        val_now = sb("val_now", [P, 2, WRITE_QUADS * JT], i32)
        cover = sb("cover", [P, WRITE_QUADS * JT])
        idx_add = sb("idx_add", [P, WRITE_QUADS * JT])
        val_add = sb("val_add", [P, WRITE_QUADS * JT])
        look_idx = sb("look_idx", [P, 3, JT], i32)
        rep_now = sb("rep_now", [P, 3, JT], i32)
        NS = 2 * GA + JT
        stats = sb("stats", [P, 2, NS, 6])
        st_a = sb("st_a", [P, NS])
        st_b = sb("st_b", [P, NS])
        st_c = sb("st_c", [P, NS])
        st_sum = sb("st_sum", [P, NS])
        st_var = sb("st_var", [P, NS])
        st_ln = sb("st_ln", [P, NS])
        st_seed = sb("st_seed", [P, NS])
        rstd = sb("rstd", [P, 2, NS])
        shift = sb("shift", [P, 2, NS])

        ps_a = ps("ps_a")
        ps_f = ps("ps_f")
        ps_h = ps("ps_h")
        ps_u = ps("ps_u")

        weights_in = sems("weights_in", 15)
        x_loaded = sems("x_loaded", 4)
        out_stored = sems("out_stored", 2)
        attr_loaded = sems("attr_loaded", 2)
        row_loaded = sems("row_loaded", 2)
        pre_loaded = sems("pre_loaded", 3)
        pre_used = sem("pre_used")
        sums_zeroed = sem("sums_zeroed")
        trash_zeroed = sem("trash_zeroed")
        const_made = sem("const_made")
        zero_made = sem("zero_made")
        iota_made = sem("iota_made")
        ident_step = sem("ident_step")
        src_f_made = sem("src_f_made")
        index_step = sem("index_step")
        spare_made = sem("spare_made")
        setup_dve = sem("setup_dve")
        setup_act = sem("setup_act")
        setup_pe = sem("setup_pe")
        setup_done = sem("setup_done")
        lone_step = sem("lone_step")
        table_written = sem("table_written")
        looked = sems("looked", 3)
        gathered = sems("gathered", 2)
        pool_waits = sem("pool_waits")
        staged = sem("staged")
        rep_saved = sem("rep_saved")
        rows_staged = sem("rows_staged")
        added = sem("added")
        stats_made = sem("stats_made")
        small_step = sem("small_step")
        var_ready = sem("var_ready")
        ln_var = sem("ln_var")
        seed_ready = sem("seed_ready")
        norm_ready = sem("norm_ready")
        edges_normed = sem("edges_normed")
        stream_normed = sem("stream_normed")
        x_copied = sem("x_copied")
        x_added = sem("x_added")
        half_summed = sem("half_summed")
        filt1_done = sem("filt1_done")
        exp_done = sem("exp_done")
        capped = sem("capped")
        log_done = sem("log_done")
        soft_ready = sem("soft_ready")
        transposed = sem("transposed")
        h_t_ready = sem("h_t_ready")
        proj_done = sem("proj_done")
        proj_ready = sem("proj_ready")
        filt2_done = sem("filt2_done")
        msg_ready = sem("msg_ready")
        y_done = sem("y_done")
        y_ready = sem("y_ready")
        same_ready = sem("same_ready")
        merged = sem("merged")
        rows_ready = sem("rows_ready")
        sum_loaded = sems("sum_loaded", 2)
        f_transposed = sem("f_transposed")
        f_exp = sem("f_exp")
        f_capped = sem("f_capped")
        f_log = sem("f_log")
        f_soft = sem("f_soft")
        f_out = sem("f_out")
        f_rows = sem("f_rows")
        out_idx_step = sem("out_idx_step")
        out_idx_made = sem("out_idx_made")
        out_added = sems("out_added", 2)

        block = ctx.enter_context(nc.Block())

        def flat(t):
            return t.rearrange("p a b -> p (a b)")

        def group_rows(dram, base):
            return dram[bass.ds(base, GR), :].rearrange("(p a) f -> p a f", a=GA)

        def group_base(g):
            return 0 if isinstance(g, int) and g == 0 else g * GR - OVERLAP

        @block.sync
        def _(sp):
            setup = [(src_i[:, :], src_cols), (dst_i[:, :], dst_cols), (weight[:, :], weight_cols),
                     (wf1_s[:, :], wf1), (w_in_s[:, :, :], w_in.rearrange("(k p) f -> p k f", p=P)),
                     (wf2_s[:, :, :], wf2.rearrange("(k p) f -> p k f", p=P)),
                     (wo1_s[:, :, :], wo1.rearrange("(k p) f -> p k f", p=P)),
                     (wo2_s[:, :, :], wo2.rearrange("(k p) f -> p k f", p=P)),
                     (bf1_c[:, :], bf1), (bf2_c[:, :], bf2), (bo1_c[:, :], bo1),
                     (bo2_row[:, :], bo2.partition_broadcast(P))]
            for n, (dst, s) in enumerate(setup):
                sp.dma_start(dst, s).then_inc(weights_in[n], 16)
            for g in range(4):
                sp.dma_start(xs[:, g], group_rows(x, group_base(g))).then_inc(x_loaded[g], 16)
            for q in range(2):
                sp.dma_start(attr[:, q], attr_t[:, bass.ts(q, QE)]).then_inc(attr_loaded[q], 16)

            def row_of(q):
                return src_rows[bass.ds(q, 1), :].partition_broadcast(P)

            for q in range(2):
                sp.dma_start(src_row[:, q], row_of(q)).then_inc(row_loaded[q], 16)

            def load_pre(n, k):
                sp.dma_start(pre_row[:, k], row_of(n)).then_inc(pre_loaded[k], 16)

            for k in range(WRITE_QUADS):
                load_pre(k, k)
            sp.wait_ge(zero_made, 1)
            sp.dma_start(out[ATOMS:OUT_ROWS, :].rearrange("(p a) f -> p a f", a=(OUT_ROWS - ATOMS) // 112),
                         zeros[0:112, :].unsqueeze(1).broadcast_to([112, (OUT_ROWS - ATOMS) // 112, F])
                         ).then_inc(trash_zeroed, 16)

            def body(q, s, zero=False, pre=0):
                static = isinstance(q, int)
                if zero:
                    sp.dma_start(sums[bass.ds(q * (ZERO_A * P), ZERO_A * P), :].rearrange("(p a) f -> p a f", a=ZERO_A),
                                 zeros[:, :].unsqueeze(1).broadcast_to([P, ZERO_A, F])).then_inc(sums_zeroed, 16)
                for h in range(2):
                    sp.wait_ge(half_summed, q * 4 + 2 * h + 2)
                    if static and q == 0 and h == 1:
                        sp.wait_ge(out_stored[0], 16)
                    sp.dma_start(group_rows(out, group_base(q * 2 + h)), hs[:, h]).then_inc(out_stored[h], 16)
                    if not static or q < QUADS - 2:
                        sp.dma_start(xs[:, 2 * s + h], group_rows(x, group_base(q * 2 + h + 4))
                                     ).then_inc(x_loaded[2 * s + h], 16)
                    if h == 0:
                        if not static or q < QUADS - 2:
                            sp.wait_ge(filt1_done, q + 1)
                            sp.dma_start(attr[:, s], attr_t[:, bass.ds((q + 2) * QE, QE)]).then_inc(attr_loaded[s], 16)
                        if not static or 0 < q < QUADS - 1:
                            sp.wait_ge(same_ready, q)
                            sp.dma_start(src_row[:, 1 - s], row_of(q + 1)).then_inc(row_loaded[1 - s], 16)
                        for k in range(pre):
                            sp.wait_ge(pre_used, (q + 1) * WRITE_QUADS + k + 1)
                            load_pre((q + 2) * WRITE_QUADS + k, k)

            for k in range(WRITE_QUADS):
                sp.wait_ge(pre_used, k + 1)
                load_pre(WRITE_QUADS + k, k)
            body(0, 0, True, WRITE_QUADS)
            body(1, 1, True, WRITE_QUADS)
            with sp.Fori(1, ZERO_QUADS // 2) as r:
                body(r * 2, 0, True, WRITE_QUADS)
                body(r * 2 + 1, 1, True, WRITE_QUADS)
            body(14, 0, False, 1)
            body(15, 1)
            with sp.Fori(EARLY // 2, 23) as r:
                body(r * 2, 0)
                body(r * 2 + 1, 1)
            body(46, 0)
            body(47, 1)
            body(48, 0)

            sp.wait_ge(added, 16 * TILES)

            def load_sums(q, s, wait=True):
                if wait:
                    sp.wait_ge(f_transposed, q - 1)
                sp.dma_start(ring[:, s], sums[bass.ds(q * QE, QE), :].rearrange("(p j) f -> p j f", j=JT)
                             ).then_inc(sum_loaded[s], 16)

            load_sums(0, 0, False)
            load_sums(1, 1, False)
            with sp.Fori(1, QUADS // 2) as r:
                load_sums(r * 2, 0)
                load_sums(r * 2 + 1, 1)
            load_sums(QUADS - 1, 0)

        @block.gpsimd
        def _(pool):
            pool.memset(all_ones[:, :], 1.0).then_inc(ident_step, 1)
            pool.memset(ident[:, :], 0.0).then_inc(ident_step, 1)
            pool.memset(earlier[:, :, :], 1.0).then_inc(ident_step, 1)
            pool.iota(edge_i[:, :], [[QE, QUADS], [1, JT]], base=0, channel_multiplier=JT).then_inc(iota_made, 1)
            pool.iota(trash_i[:, :], [[P, 2 * JT]], base=OUT_TRASH, channel_multiplier=1).then_inc(iota_made, 1)
            pool.iota(spare_table[:, :], [[0, QUADS], [P, JT]], base=TABLE_TRASH, channel_multiplier=1).then_inc(iota_made, 1)
            pool.iota(spare_sum[:, :], [[-QE, QUADS], [P - 1, JT]], base=SUM_TRASH, channel_multiplier=1 - JT
                      ).then_inc(iota_made, 1)
            pool.wait_ge(ident_step, 3)
            pool.affine_select(out=ident[:, :], in_=ident[:, :], compare_op=ALU.not_equal, fill=1.0, base=0,
                               pattern=[[-1, P]], channel_multiplier=1).then_inc(const_made, 1)
            last = earlier[:, JT - 1, :]
            pool.affine_select(out=last, in_=last, compare_op=ALU.is_gt, fill=0.0, base=0,
                               pattern=[[-1, P]], channel_multiplier=1).then_inc(const_made, 1)

            def at(idx):
                return bass.IndirectOffsetOnAxis(ap=idx, axis=0)

            def wait_alone(sem, value):
                pool.wait_ge(sem, value)
                pool.sem_inc(pool_waits, 1)

            def gather(idx, s, j):
                pool.indirect_dma_start(xg[:, s, j], None, x[:, :], at(idx)).then_inc(gathered[s], 16)

            def write_table(n, s, k):
                if not (isinstance(n, int) and n == 0):
                    wait_alone(table_written, n * (16 * JT))
                for j in range(JT):
                    c = k * JT + j
                    pool.indirect_dma_start(table[:, :], at(idx_now[:, s, c:c + 1]), val_now[:, s, c:c + 1], None
                                            ).then_inc(table_written, 16)

            def look(idx, k):
                for j in range(JT):
                    pool.indirect_dma_start(rep_now[:, k, j:j + 1], None, table[:, :], at(idx[:, j:j + 1])
                                            ).then_inc(looked[k], 16)

            def look_again(n, k):
                wait_alone(rep_saved, n - 2)
                look(look_idx[:, k], k)

            def add_rows(n, k, times):
                if not (isinstance(n, int) and n == 0):
                    wait_alone(added, n * (16 * JT))
                wait_alone(looked[k], times * (16 * JT))
                wait_alone(rows_staged, n + 1)
                for j in range(JT):
                    pool.indirect_dma_start(sums[:, :], at(rep_now[:, k, j:j + 1]), row_now[:, k, j], None,
                                            compute_op=ALU.add).then_inc(added, 16)

            def gather_pair(q, s, b):
                if b == 0:
                    wait_alone(transposed, q + 1)
                for j in (2 * b, 2 * b + 1):
                    gather(dst_now[:, s, j:j + 1], s, j)

            pool.wait_ge(weights_in[1], 16)
            for q in range(2):
                for j in range(JT):
                    gather(dst_i[:, q * JT + j:q * JT + j + 1], q, j)

            def early(q, s):
                wait_alone(staged, q + 1)
                write_table(q * 3, s, 0)
                gather_pair(q, s, 0)
                write_table(q * 3 + 1, s, 1)
                gather_pair(q, s, 1)
                write_table(q * 3 + 2, s, 2)

            early(0, 0)
            early(1, 1)
            with pool.Fori(1, EARLY // 2) as r:
                early(r * 2, 0)
                early(r * 2 + 1, 1)

            pool.wait_ge(staged, EARLY + 1)
            write_table(QUADS - 1, 0, 0)
            gather_pair(EARLY, 0, 0)
            gather_pair(EARLY, 0, 1)
            pool.wait_ge(table_written, 16 * TILES)
            for k in range(3):
                look(table_idx[:, k * JT:(k + 1) * JT], k)
            pool.wait_ge(sums_zeroed, 16 * ZERO_QUADS)
            add_rows(0, 0, 1)

            def unit(n, k, times, more=True):
                add_rows(n, k, times)
                if more:
                    look_again(n + 2, (k + 2) % 3)

            def fetch(q, s):
                wait_alone(staged, q + 1)
                gather_pair(q, s, 0)
                gather_pair(q, s, 1)

            fetch(17, 1)
            unit(1, 1, 1)
            unit(2, 2, 1)
            with pool.Fori(9, 22) as r:
                fetch(r * 2, 0)
                unit(r * 3 - 24, 0, r - 7)
                fetch(r * 2 + 1, 1)
                unit(r * 3 - 23, 1, r - 7)
                unit(r * 3 - 22, 2, r - 7)
            for q in (44, 45, 46):
                fetch(q, q % 2)
                unit(q - 2, (q - 2) % 3, (q - 2) // 3 + 1)
            for n in range(45, QUADS):
                unit(n, n % 3, n // 3 + 1, n < QUADS - 2)

            pool.wait_ge(out_idx_made, 1)
            for h in range(2):
                pool.wait_ge(out_stored[h], 16 * QUADS)
            pool.wait_ge(trash_zeroed, 16)

            def add_out(q, s, wait=True):
                wait_alone(f_rows, q + 1)
                if wait:
                    wait_alone(out_added[s], (q - s) * 32)
                for j in range(JT):
                    pool.indirect_dma_start(out[:, :], at(dst_now[:, s, j:j + 1]), ring[:, 4 + s, j], None,
                                            compute_op=ALU.add).then_inc(out_added[s], 16)

            add_out(0, 0, False)
            add_out(1, 1, False)
            with pool.Fori(1, QUADS // 2) as r:
                add_out(r * 2, 0)
                add_out(r * 2 + 1, 1)
            add_out(QUADS - 1, 0)
            pool.wait_ge(out_added[0], 64 * (QUADS // 2 + 1))
            pool.wait_ge(out_added[1], 64 * (QUADS // 2))

        @block.scalar
        def _(act):
            act.preload_act_table_set("natural_log_exp_and_others")
            act.wait_ge(weights_in[10], 16)
            act.activation(sp0[:, :], bo1_c[:, :], ACT.Exp).then_inc(setup_act, 1)
            act.wait_ge(setup_dve, 2)
            act.activation(sp0[:, :], sp0[:, :], ACT.Ln, bias=1.0).then_inc(setup_act, 1)

            def seed(n):
                act.wait_ge(var_ready, n)
                act.activation(st_ln[:, :], st_var[:, :], ACT.Ln).then_inc(ln_var, 1)
                act.wait_ge(ln_var, n)
                act.activation(st_seed[:, :], st_ln[:, :], ACT.Exp, scale=-0.5).then_inc(seed_ready, 1)

            seed(1)

            def stage_rows(n, k):
                act.wait_ge(rows_ready, n + 1)
                if not (isinstance(n, int) and n < 3):
                    act.wait_ge(added, (n - 2) * (16 * JT))
                act.activation(row_now[:, k], ring[:, bass.ds(n % RING, 1)].squeeze(1), ACT.Copy
                               ).then_inc(rows_staged, 1)

            def keep_rows(q, slot):
                act.wait_ge(merged, q + 1)
                dst = ring[:, bass.ds(slot, 1)].rearrange("p o j f -> p (o j f)")
                for k in range(KC):
                    ins = act.activation(dst[:, bass.ts(k, QE)], ps_f[:, k], ACT.Copy)
                ins.then_inc(rows_ready, 1)

            def copy_y(q):
                act.wait_ge(y_done, q + 1)
                if not (isinstance(q, int) and q == 0):
                    act.wait_ge(merged, q)
                y_flat = flat(y_rows[:, :, :])
                for k in range(KC):
                    ins = act.activation(y_flat[:, bass.ts(k, QE)], ps_h[:, k], ACT.Copy)
                ins.then_inc(y_ready, 1)

            def copy_proj(q):
                act.wait_ge(proj_done, q + 1)
                if not (isinstance(q, int) and q == 0):
                    act.wait_ge(y_done, q)
                for k in range(KC):
                    ins = act.activation(msg[:, k], ps_h[:, k], ACT.Copy)
                ins.then_inc(proj_ready, 1)

            def body(q, s, slot=None, stage=(), last=False):
                static = isinstance(q, int)

                def norm_stream(half):
                    h, a0 = half // 2, (half % 2) * 4
                    if half % 2 == 0 and not (static and q == 0):
                        act.wait_ge(out_stored[h], q * 16)
                    for a in range(a0, a0 + 4):
                        c = h * GA + a
                        ins = act.activation(hs[:, h, a], xs[:, 2 * s + h, a], ACT.Relu,
                                             bias=shift[:, s, c:c + 1], scale=rstd[:, s, c:c + 1])
                    ins.then_inc(stream_normed, 1)

                if not static or q > 1:
                    keep_rows(q - 2, slot)
                act.wait_ge(norm_ready, q + 1)
                for j in range(JT):
                    c = 2 * GA + j
                    ins = act.activation(xg[:, s, j], xg[:, s, j], ACT.Relu,
                                         bias=shift[:, s, c:c + 1], scale=rstd[:, s, c:c + 1])
                ins.then_inc(edges_normed, 1)
                norm_stream(0)
                if not (static and q == 0):
                    copy_proj(q - 1)
                norm_stream(1)
                for n, k in stage:
                    stage_rows(n, k)
                act.wait_ge(filt1_done, q + 1)
                if not (static and q == 0):
                    act.wait_ge(filt2_done, q)
                for k in range(KC):
                    ins = act.activation(soft[:, k], ps_a[:, k], ACT.Exp, bias=bf1_c[:, k:k + 1])
                ins.then_inc(exp_done, 1)
                norm_stream(2)
                act.wait_ge(capped, q + 1)
                act.activation(flat(soft[:, :, :]), flat(soft[:, :, :]), ACT.Ln, bias=1.0).then_inc(log_done, 1)
                if not (static and q == 0):
                    copy_y(q - 1)
                act.wait_ge(transposed, q + 1)
                if not (static and q == 0):
                    act.wait_ge(proj_done, q)
                for k in range(KC):
                    ins = act.activation(h_t[:, k], ps_h[:, k], ACT.Copy)
                ins.then_inc(h_t_ready, 1)
                if not last:
                    seed(q + 2)
                norm_stream(3)

            body(0, 0)
            body(1, 1)
            with act.Fori(1, EARLY // 2) as r:
                body(r * 2, 0, r * 2 - 2)
                body(r * 2 + 1, 1, r * 2 - 1)
            body(16, 0, 14, ((0, 0),))
            body(17, 1, 15, ((1, 1), (2, 2)))
            with act.Fori(9, 22) as r:
                body(r * 2, 0, (r * 2 - 2) % RING, ((r * 3 - 24, 0),))
                body(r * 2 + 1, 1, (r * 2 - 1) % RING, ((r * 3 - 23, 1), (r * 3 - 22, 2)))
            for q in range(44, QUADS):
                body(q, q % 2, (q - 2) % RING, ((q - 2, (q - 2) % 3),), last=(q == QUADS - 1))
            keep_rows(QUADS - 2, (QUADS - 2) % RING)
            stage_rows(QUADS - 2, (QUADS - 2) % 3)
            copy_proj(QUADS - 1)
            copy_y(QUADS - 1)
            keep_rows(QUADS - 1, (QUADS - 1) % RING)
            stage_rows(QUADS - 1, (QUADS - 1) % 3)

            def f_first(q, s, wait=True):
                act.wait_ge(f_transposed, q + 1)
                if wait:
                    act.wait_ge(f_soft, q - 1)
                for k in range(KC):
                    ins = act.activation(flat(ring[:, 2 + s])[:, bass.ts(k, QE)], (ps_f, ps_h)[s][:, k], ACT.Exp,
                                         bias=bo1_c[:, k:k + 1])
                ins.then_inc(f_exp, 1)

            def f_second(q, s):
                act.wait_ge(f_capped, q + 1)
                act.activation(flat(ring[:, 2 + s]), flat(ring[:, 2 + s]), ACT.Ln, bias=1.0).then_inc(f_log, 1)

            f_first(0, 0, False)
            f_first(1, 1, False)
            f_second(0, 0)
            f_second(1, 1)
            with act.Fori(1, QUADS // 2) as r:
                f_first(r * 2, 0)
                f_second(r * 2, 0)
                f_first(r * 2 + 1, 1)
                f_second(r * 2 + 1, 1)
            f_first(QUADS - 1, 0)
            f_second(QUADS - 1, 0)

        @block.tensor
        def _(pe):
            pe.wait_ge(const_made, 2)
            for n in range(3, 8):
                pe.wait_ge(weights_in[n], 16)
            pe.wait_ge(setup_dve, 1)
            for c in range(KC):
                for k in range(KC):
                    ins = pe.matmul(ps_f[:, 0, c:c + 1], wf2_s[:, k, bass.ts(c, P)], neg_log2[:, :],
                                    start=(k == 0), stop=(k == KC - 1))
            ins.then_inc(setup_pe, 1)
            pe.wait_ge(setup_dve, 6)
            for v in range(2):
                for k in range(KC):
                    ins = pe.matmul(ps_h[:, v, 0:F], y_rows[:, k, v * P:(v + 1) * P], wo2_s[:, k],
                                    start=(k == 0), stop=(k == KC - 1))
            ins.then_inc(setup_pe, 1)
            pe.wait_ge(lone_step, 6)

            def copy_x(q, s, b, before):
                h, a0 = b // 2, (b % 2) * 4
                if b % 2 == 0:
                    pe.wait_ge(x_loaded[2 * s + h], q * 8 + (16 if s == 0 else 8))
                if not (isinstance(q, int) and q * 4 + before <= 0):
                    pe.wait_ge(half_summed, q * 4 + before)
                for k in range(2):
                    pe.matmul(ps_u[:, k], ident[:, :], xs[:, 2 * s + h, a0 + 2 * k:a0 + 2 * k + 2]
                              .rearrange("p a f -> p (a f)"), start=True, stop=False)
                    ins = pe.matmul(ps_u[:, k], all_ones[:, :], flat(lone_parts[:, :, :]), start=False, stop=True)
                ins.then_inc(x_copied, 1)

            def body(q, s, copies=((), (), ()), front=True, back=True):
                if back:
                    pe.wait_ge(h_t_ready, q)
                    for c in range(KC):
                        for k in range(KC):
                            ins = pe.matmul(ps_h[:, c], w_in_s[:, k, bass.ts(c, P)], h_t[:, k],
                                            start=(k == 0), stop=(k == KC - 1))
                    ins.then_inc(proj_done, 1)
                for b, before in copies[0]:
                    copy_x(q, s, b, before)
                if back:
                    pe.wait_ge(soft_ready, q)
                    if not (isinstance(q, int) and q == 1):
                        pe.wait_ge(rows_ready, q - 1)
                    for c in range(KC):
                        for k in range(KC):
                            ins = pe.matmul(ps_f[:, c], wf2_s[:, k, bass.ts(c, P)], soft[:, k],
                                            start=(k == 0), stop=(k == KC - 1))
                    ins.then_inc(filt2_done, 1)
                if front:
                    pe.wait_ge(attr_loaded[s], q * 8 + (16 if s == 0 else 8))
                    for c in range(KC):
                        ins = pe.matmul(ps_a[:, c], wf1_s[:, bass.ts(c, P)], attr[:, s], start=True, stop=True)
                    ins.then_inc(filt1_done, 1)
                for b, before in copies[1]:
                    copy_x(q, s, b, before)
                if back:
                    pe.wait_ge(msg_ready, q)
                    rows = ps_h[:, :, :].rearrange("p k (a f) -> p (k a) f", f=F)
                    for j in range(JT):
                        for k in range(KC):
                            ins = pe.matmul(rows[:, j], msg[:, k, bass.ts(j, P)], wo1_s[:, k],
                                            start=(k == 0), stop=(k == KC - 1))
                    ins.then_inc(y_done, 1)
                for b, before in copies[2]:
                    copy_x(q, s, b, before)
                if back:
                    pe.wait_ge(y_ready, q)
                if front:
                    pe.wait_ge(edges_normed, q + 1)
                    for k in range(KC):
                        for j in range(JT):
                            ins = pe.transpose(ps_h[:, k, bass.ts(j, P)], xg[:, s, j, bass.ts(k, P)], ident[:, :])
                    ins.then_inc(transposed, 1)
                if back:
                    pe.wait_ge(same_ready, q)
                    rows = ps_f[:, :, :].rearrange("p k (a f) -> p (k a) f", f=F)
                    for i in range(JT):
                        for j in range(i, JT):
                            ins = pe.matmul(rows[:, i], same[:, j, bass.ts(i, P)], y_rows[:, j],
                                            start=(j == i), stop=(j == JT - 1))
                    ins.then_inc(merged, 1)

            early = ((0, -1),), ((1, 1),), ((2, 2),)
            body(0, 0, early, back=False)
            body(1, 1, early)
            with pe.Fori(1, EARLY // 2) as r:
                body(r * 2, 0, early)
                body(r * 2 + 1, 1, early)
            with pe.Fori(EARLY // 2, QUADS // 2) as r:
                body(r * 2, 0, ((), ((1, -1),), ()))
                body(r * 2 + 1, 1, ((), ((1, -2),), ((2, 2),)))
            body(QUADS - 1, 0, ((), ((1, -1),), ()))
            body(QUADS, 1, front=False)

            def f_turn(q, s, wait=True):
                pe.wait_ge(sum_loaded[s], q * 8 + (16 if s == 0 else 8))
                if wait:
                    pe.wait_ge(f_soft, q - 1)
                for k in range(KC):
                    for j in range(JT):
                        ins = pe.transpose((ps_f, ps_h)[s][:, k, bass.ts(j, P)], ring[:, s, j, bass.ts(k, P)], ident[:, :])
                ins.then_inc(f_transposed, 1)

            def f_mul(q, s, wait=True):
                pe.wait_ge(f_soft, q + 1)
                if wait:
                    pe.wait_ge(f_rows, q - 1)
                sp_t = flat(ring[:, 6 + s]).rearrange("p (k e) -> p k e", k=KC)
                rows = (ps_a, ps_u)[s][:, :, :].rearrange("p k (a f) -> p (k a) f", f=F)
                for j in range(JT):
                    for k in range(KC):
                        ins = pe.matmul(rows[:, j], sp_t[:, k, bass.ts(j, P)], wo2_s[:, k],
                                        start=(k == 0), stop=(k == KC - 1))
                ins.then_inc(f_out, 1)

            pe.wait_ge(rows_ready, QUADS)
            f_turn(0, 0, False)
            f_turn(1, 1, False)
            f_turn(2, 0)
            f_mul(0, 0, False)
            f_turn(3, 1)
            f_mul(1, 1, False)
            with pe.Fori(2, QUADS // 2) as r:
                f_turn(r * 2, 0)
                f_mul(r * 2 - 2, 0)
                f_turn(r * 2 + 1, 1)
                f_mul(r * 2 - 1, 1)
            f_turn(QUADS - 1, 0)
            f_mul(QUADS - 3, 0)
            f_mul(QUADS - 2, 1)
            f_mul(QUADS - 1, 0)

        @block.vector
        def _(dve):
            dve.memset(neg_log2[:, :], -LOG2).then_inc(setup_dve, 1)
            dve.memset(ones[:, :], 1.0)
            dve.memset(zeros[:, :], 0.0).then_inc(zero_made, 1)
            dve.wait_ge(weights_in[0], 16)
            dve.tensor_copy(src_f[:, :], src_i[:, :]).then_inc(src_f_made, 1)
            dve.wait_ge(src_f_made, 1)
            dve.wait_ge(iota_made, 4)
            dve.tensor_tensor(spare_less_src[:, :], spare_table[:, :], src_f[:, :], ALU.subtract).then_inc(spare_made, 1)
            dve.wait_ge(spare_made, 1)
            dve.wait_ge(const_made, 2)
            dve.wait_ge(weights_in[1], 16)

            def cover_quad(n, k, wait, loads):
                dve.wait_ge(pre_loaded[k], loads * 16)
                if wait:
                    dve.wait_ge(pre_used, n)
                at = 0
                for j in range(JT):
                    w = (j + 1) * P
                    ins = dve.scalar_tensor_tensor(out=hits[:, at:at + w], in0=pre_row[:, k, 0:w],
                                                   scalar=src_f[:, bass.ds(n * JT + j, 1)],
                                                   in1=earlier[:, JT - 1 - j:JT].rearrange("p a i -> p (a i)"),
                                                   op0=ALU.is_equal, op1=ALU.mult,
                                                   accum_out=cover[:, k * JT + j:k * JT + j + 1])
                    at += w
                ins.then_inc(pre_used, 1)

            def plan(q, s, n, count=WRITE_QUADS):
                w = count * JT
                cols = bass.ds(n * JT, w)
                dve.wait_ge(pre_used, n + count)
                dve.scalar_tensor_tensor(out=idx_add[:, 0:w], in0=cover[:, 0:w], scalar=1.0, in1=spare_less_src[:, cols],
                                         op0=ALU.min, op1=ALU.mult).then_inc(index_step, 1)
                dve.scalar_tensor_tensor(out=val_add[:, 0:w], in0=cover[:, 0:w], scalar=1.0, in1=spare_sum[:, cols],
                                         op0=ALU.min, op1=ALU.mult).then_inc(index_step, 1)
                if not (isinstance(q, int) and q < 2):
                    dve.wait_ge(table_written, (q - 1) * (16 * JT * WRITE_QUADS))
                dve.wait_ge(index_step, q * 3 + 1)
                dve.tensor_tensor(idx_now[:, s, 0:w], idx_add[:, 0:w], src_f[:, cols], ALU.add).then_inc(index_step, 1)
                dve.wait_ge(index_step, q * 3 + 2)
                dve.tensor_tensor(val_now[:, s, 0:w], val_add[:, 0:w], edge_i[:, cols], ALU.add)
                dve.wait_ge(index_step, q * 3 + 3)
                dve.tensor_copy(table_idx[:, cols], idx_now[:, s, 0:w]).then_inc(staged, 1)

            def stage_dst(q, s):
                return dve.tensor_copy(dst_now[:, s], dst_i[:, bass.ds((q + 2) * JT, JT)])

            for k in range(WRITE_QUADS):
                cover_quad(k, k, k > 0, 1)
            stage_dst(0, 0)
            plan(0, 0, 0)

            dve.wait_ge(setup_act, 1)
            dve.tensor_scalar(sp0[:, :], sp0[:, :], EXP_CAP, None, ALU.min).then_inc(setup_dve, 1)
            dve.wait_ge(setup_act, 2)
            dve.tensor_tensor(sp0[:, :], sp0[:, :], bo1_c[:, :], ALU.max).then_inc(setup_dve, 1)
            dve.wait_ge(setup_dve, 3)
            dve.tensor_scalar(sp0_shift[:, :], sp0[:, :], -LOG2, None, ALU.add).then_inc(setup_dve, 1)
            dve.wait_ge(setup_dve, 4)
            for v, s0 in enumerate((sp0, sp0_shift)):
                for k in range(KC):
                    ins = dve.tensor_scalar(y_rows[:, k, v * P:(v + 1) * P], ones[:, :], s0[:, k:k + 1], None, ALU.mult)
                ins.then_inc(setup_dve, 1)
            dve.wait_ge(setup_pe, 1)
            dve.wait_ge(weights_in[9], 16)
            dve.tensor_tensor(filt_bias[:, :], ps_f[:, 0, 0:KC], bf2_c[:, :], ALU.add)
            dve.wait_ge(setup_pe, 2)
            dve.wait_ge(weights_in[11], 16)
            dve.tensor_copy(lean_row[:, :], ps_h[:, 0, 0:F])
            dve.tensor_tensor(lone_row[:, :], ps_h[:, 1, 0:F], bo2_row[:, :], ALU.add).then_inc(setup_done, 1)
            dve.wait_ge(setup_done, 1)
            dve.wait_ge(pre_used, WRITE_QUADS)
            dve.tensor_copy(lone_hi, lone_row[:, :]).then_inc(lone_step, 1)
            dve.wait_ge(lone_step, 1)
            dve.tensor_tensor(lone_rest, lone_row[:, :], lone_hi, ALU.subtract)
            dve.tensor_scalar(lone_sum, lone_hi, ident[:, 0:1], None, ALU.mult).then_inc(lone_step, 1)
            dve.wait_ge(lone_step, 2)
            dve.tensor_copy(lone_mid, lone_rest).then_inc(lone_step, 1)
            dve.wait_ge(lone_step, 3)
            dve.tensor_tensor(lone_low, lone_rest, lone_mid, ALU.subtract).then_inc(lone_step, 1)
            dve.wait_ge(lone_step, 4)
            dve.scalar_tensor_tensor(out=lone_rest, in0=lone_mid, scalar=ident[:, 1:2], in1=lone_sum,
                                     op0=ALU.mult, op1=ALU.add).then_inc(lone_step, 1)
            dve.wait_ge(lone_step, 5)
            for a in range(2):
                ins = dve.scalar_tensor_tensor(out=lone_parts[:, a], in0=lone_low, scalar=ident[:, 2:3], in1=lone_rest,
                                               op0=ALU.mult, op1=ALU.add)
            ins.then_inc(lone_step, 1)
            for n in (2, 8):
                dve.wait_ge(weights_in[n], 16)

            def stream_stats(q, s, h):
                dve.wait_ge(x_loaded[2 * s + h], q * 8 + (16 if s == 0 else 8))
                for a in range(GA):
                    ins = dve.bn_stats(stats[:, s, h * GA + a], xs[:, 2 * s + h, a])
                if h == 1:
                    ins.then_inc(stats_made, 1)

            def edge_stats(q, s):
                dve.wait_ge(gathered[s], q * 32 + (64 if s == 0 else 32))
                for j in range(JT):
                    dve.bn_stats(stats[:, s, 2 * GA + j], xg[:, s, j])

            def variance(q, s):
                def wait(n):
                    dve.wait_ge(small_step, q * 8 + n)
                dve.wait_ge(stats_made, q + 1)
                me, mo = stats[:, s, :, 1], stats[:, s, :, 4]
                dve.tensor_tensor(st_a[:, :], me, mo, ALU.subtract).then_inc(small_step, 1)
                dve.tensor_tensor(st_b[:, :], stats[:, s, :, 2], stats[:, s, :, 5], ALU.add).then_inc(small_step, 1)
                dve.tensor_tensor(st_sum[:, :], me, mo, ALU.add)
                wait(1)
                dve.scalar_tensor_tensor(out=st_c[:, :], in0=st_a[:, :], scalar=0.25, in1=st_a[:, :],
                                         op0=ALU.mult, op1=ALU.mult).then_inc(small_step, 1)
                wait(3)
                dve.scalar_tensor_tensor(out=st_a[:, :], in0=st_b[:, :], scalar=1.0 / F, in1=st_c[:, :],
                                         op0=ALU.mult, op1=ALU.add).then_inc(small_step, 1)
                wait(4)
                dve.tensor_scalar(st_var[:, :], st_a[:, :], EPS, None, ALU.add).then_inc(var_ready, 1)

            def norm(q, s):
                def wait(n):
                    dve.wait_ge(small_step, q * 8 + n)
                dve.wait_ge(seed_ready, q + 1)
                dve.tensor_tensor(st_b[:, :], st_seed[:, :], st_seed[:, :], ALU.mult).then_inc(small_step, 1)
                wait(5)
                dve.tensor_tensor(st_c[:, :], st_b[:, :], st_var[:, :], ALU.mult).then_inc(small_step, 1)
                wait(6)
                dve.tensor_scalar(st_a[:, :], st_c[:, :], -0.5, 1.5, ALU.mult, ALU.add).then_inc(small_step, 1)
                wait(7)
                dve.tensor_tensor(rstd[:, s], st_seed[:, :], st_a[:, :], ALU.mult).then_inc(small_step, 1)
                wait(8)
                dve.scalar_tensor_tensor(out=shift[:, s], in0=st_sum[:, :], scalar=-0.5, in1=rstd[:, s],
                                         op0=ALU.mult, op1=ALU.mult).then_inc(norm_ready, 1)

            stream_stats(0, 0, 0)
            edge_stats(0, 0)
            stream_stats(0, 0, 1)
            variance(0, 0)
            norm(0, 0)

            def keep_reps(n, k, times, more=True):
                dve.wait_ge(looked[k], times * (16 * JT))
                ins = dve.tensor_copy(rep_i[:, bass.ds(n * JT, JT)], rep_now[:, k])
                if more:
                    ins = dve.tensor_copy(look_idx[:, k], table_idx[:, bass.ds((n + 3) * JT, JT)])
                ins.then_inc(rep_saved, 1)

            def match(q, s):
                dve.wait_ge(row_loaded[s], q * 8 + (16 if s == 0 else 8))
                if not (isinstance(q, int) and q == 0):
                    dve.wait_ge(merged, q)
                for j in range(JT):
                    w = (j + 1) * P
                    ins = dve.tensor_scalar(same[:, j, 0:w], src_row[:, s, 0:w],
                                            src_f[:, bass.ds(q * JT + j, 1)], weight[:, bass.ds(q * JT + j, 1)],
                                            ALU.is_equal, ALU.mult)
                ins.then_inc(same_ready, 1)

            def message(q):
                dve.wait_ge(filt2_done, q + 1)
                dve.wait_ge(proj_ready, q + 1)
                for k in range(KC):
                    ins = dve.scalar_tensor_tensor(out=msg[:, k], in0=ps_f[:, k], scalar=filt_bias[:, k:k + 1],
                                                   in1=msg[:, k], op0=ALU.add, op1=ALU.mult)
                ins.then_inc(msg_ready, 1)

            def body(q, s, halves, write=0, keep=(), last=False, fetch=True):
                static = isinstance(q, int)

                def combine(b):
                    h, a0 = b // 2, (b % 2) * 4
                    out_rows, x_rows = hs[:, h, a0:a0 + 4], xs[:, 2 * s + h, a0:a0 + 4]
                    dve.wait_ge(stream_normed, q * 4 + b + 1)
                    by_tensor, count = halves[b]
                    if by_tensor:
                        dve.wait_ge(x_copied, count)
                        dve.tensor_tensor(flat(out_rows), flat(out_rows), flat(ps_u[:, :, :]), ALU.add
                                          ).then_inc(half_summed, 1)
                    else:
                        dve.tensor_tensor(flat(out_rows), flat(out_rows), flat(x_rows), ALU.add).then_inc(x_added, 1)
                        dve.wait_ge(x_added, count)
                        dve.tensor_tensor(out_rows, out_rows, lone_row[:, :].unsqueeze(1).broadcast_to([P, 4, F]),
                                          ALU.add).then_inc(half_summed, 1)

                if not static or q > 0:
                    match(q - 1, 1 - s)
                if not last:
                    stream_stats(q + 1, 1 - s, 0)
                combine(0)
                if not static or q > 0:
                    message(q - 1)
                if not last:
                    edge_stats(q + 1, 1 - s)
                combine(1)
                dve.wait_ge(exp_done, q + 1)
                dve.tensor_scalar(flat(soft[:, :, :]), flat(soft[:, :, :]), EXP_CAP, None, ALU.min).then_inc(capped, 1)
                if not last:
                    stream_stats(q + 1, 1 - s, 1)
                    variance(q + 1, 1 - s)
                dve.wait_ge(log_done, q + 1)
                for k in range(KC):
                    ins = dve.scalar_tensor_tensor(out=soft[:, k], in0=ps_a[:, k], scalar=bf1_c[:, k:k + 1],
                                                   in1=soft[:, k], op0=ALU.add, op1=ALU.max)
                ins.then_inc(soft_ready, 1)
                if not last:
                    if fetch:
                        ins = stage_dst(q + 1, 1 - s)
                    if write:
                        for k in range(write):
                            cover_quad((q + 1) * WRITE_QUADS + k, k, True, q + 2)
                        plan(q + 1, 1 - s, (q + 1) * WRITE_QUADS, write)
                    elif fetch:
                        ins.then_inc(staged, 1)
                combine(2)
                for n, k, times in keep:
                    keep_reps(n, k, times, more=not (isinstance(n, int) and n >= QUADS - 3))
                if not last:
                    norm(q + 1, 1 - s)
                combine(3)

            def early_copies(q):
                return (True, q * 3 + 1), (True, q * 3 + 2), (True, q * 3 + 3), (False, q + 1)

            def even_copies(r):
                copied, added_to = (r - EARLY // 2) * 3 + EARLY * 3, (r - EARLY // 2) * 5 + EARLY
                return (False, added_to + 1), (True, copied + 1), (False, added_to + 2), (False, added_to + 3)

            def odd_copies(r):
                copied, added_to = (r - EARLY // 2) * 3 + EARLY * 3 + 1, (r - EARLY // 2) * 5 + EARLY + 3
                return (False, added_to + 1), (True, copied + 1), (True, copied + 2), (False, added_to + 2)

            body(0, 0, early_copies(0), WRITE_QUADS)
            body(1, 1, early_copies(1), WRITE_QUADS)
            with dve.Fori(1, EARLY // 2 - 1) as r:
                body(r * 2, 0, early_copies(r * 2), WRITE_QUADS)
                body(r * 2 + 1, 1, early_copies(r * 2 + 1), WRITE_QUADS)
            body(14, 0, early_copies(14), WRITE_QUADS)
            body(15, 1, early_copies(15), 1)
            body(16, 0, even_copies(8), keep=((0, 0, 1),))
            body(17, 1, odd_copies(8), keep=((1, 1, 1), (2, 2, 1)))
            with dve.Fori(9, 22) as r:
                body(r * 2, 0, even_copies(r), keep=((r * 3 - 24, 0, r - 7),))
                body(r * 2 + 1, 1, odd_copies(r), keep=((r * 3 - 23, 1, r - 7), (r * 3 - 22, 2, r - 7)))
            for q in range(44, QUADS):
                body(q, q % 2, (even_copies, odd_copies)[q % 2](q // 2), keep=((q - 2, (q - 2) % 3, (q - 2) // 3 + 1),),
                     last=(q == QUADS - 1), fetch=(q < QUADS - 3))
            match(QUADS - 1, 0)
            message(QUADS - 1)
            for n in (QUADS - 2, QUADS - 1):
                keep_reps(n, n % 3, n // 3 + 1, more=False)

            whole = TILES // 8 * 8

            def with_spares(o, i, op):
                dve.tensor_tensor(o[:, 0:whole].rearrange("p (a b) -> p a b", b=8),
                                  i[:, 0:whole].rearrange("p (a b) -> p a b", b=8),
                                  trash_i[:, :].unsqueeze(1).broadcast_to([P, TILES // 8, 8]), op)
                return dve.tensor_tensor(o[:, whole:TILES], i[:, whole:TILES], trash_i[:, 0:TILES - whole], op)

            dve.wait_ge(y_done, QUADS)
            dve.wait_ge(rep_saved, QUADS)
            is_rep, gain = msg[:, 0, 0:TILES], msg[:, 1, 0:TILES]
            dve.tensor_tensor(is_rep, rep_i[:, :], edge_i[:, :], ALU.is_equal)
            with_spares(gain, src_f, ALU.subtract).then_inc(out_idx_step, 1)
            dve.wait_ge(out_idx_step, 1)
            dve.tensor_tensor(gain, gain, is_rep, ALU.mult).then_inc(out_idx_step, 1)
            dve.wait_ge(out_idx_step, 2)
            with_spares(out_idx, gain, ALU.add).then_inc(out_idx_made, 1)
            dve.wait_ge(out_idx_made, 1)

            def f_cap(q, s):
                dve.wait_ge(f_exp, q + 1)
                e = flat(ring[:, 2 + s])
                dve.tensor_scalar(e, e, EXP_CAP, None, ALU.min).then_inc(f_capped, 1)

            def f_max(q, s, wait=True):
                dve.wait_ge(f_log, q + 1)
                if wait:
                    dve.wait_ge(f_out, q - 1)
                for k in range(KC):
                    half = bass.ts(k, QE)
                    ins = dve.scalar_tensor_tensor(out=flat(ring[:, 6 + s])[:, half], in0=(ps_f, ps_h)[s][:, k],
                                                   scalar=bo1_c[:, k:k + 1], in1=flat(ring[:, 2 + s])[:, half],
                                                   op0=ALU.add, op1=ALU.max)
                ins.then_inc(f_soft, 1)

            def f_sub(q, s, wait=True):
                dve.wait_ge(f_out, q + 1)
                if wait:
                    dve.wait_ge(out_added[s], (q - s) * 32)
                dve.tensor_copy(dst_now[:, s], out_idx[:, bass.ds(q * JT, JT)])
                rows = (ps_a, ps_u)[s][:, :, :].rearrange("p k (a f) -> p (k a) f", f=F)
                dve.tensor_tensor(ring[:, 4 + s], rows, lean_row[:, :].unsqueeze(1).broadcast_to([P, JT, F]),
                                  ALU.subtract).then_inc(f_rows, 1)

            f_cap(0, 0)
            f_cap(1, 1)
            f_max(0, 0, False)
            f_max(1, 1, False)
            f_cap(2, 0)
            f_sub(0, 0, False)
            f_max(2, 0)
            f_cap(3, 1)
            f_sub(1, 1, False)
            f_max(3, 1)
            with dve.Fori(2, QUADS // 2) as r:
                f_cap(r * 2, 0)
                f_sub(r * 2 - 2, 0)
                f_max(r * 2, 0)
                f_cap(r * 2 + 1, 1)
                f_sub(r * 2 - 1, 1)
                f_max(r * 2 + 1, 1)
            f_cap(QUADS - 1, 0)
            f_sub(QUADS - 3, 0)
            f_max(QUADS - 1, 0)
            f_sub(QUADS - 2, 1)
            f_sub(QUADS - 1, 0)


def kernel(**inputs):
    import numpy as np
    import concourse.bacc as bacc
    from concourse import mybir as mb
    from concourse.bass_utils import run_bass_kernel_spmd as run

    nc = bacc.Bacc("TRN2", target_bir_lowering=False, num_devices=1)
    a = {k: np.asarray(v) for k, v in inputs.items()}

    def padded(v, fill):
        return np.concatenate([v, np.full((PAD_EDGES - EDGES,) + v.shape[1:], fill, v.dtype)])

    def cols(v, fill):
        return np.ascontiguousarray(padded(v, fill).reshape(QUADS, P, JT).transpose(1, 0, 2).reshape(P, TILES))

    def by_tile(v, fill):
        v = padded(v, fill)
        return v.reshape((QUADS, P, JT) + v.shape[1:]).swapaxes(1, 2).reshape((QUADS, QE) + v.shape[1:])

    def chunked(v):
        return np.ascontiguousarray(v.reshape(KC, P).T)

    arrays = {
        "x": np.ascontiguousarray(a["x"]),
        "src_cols": cols(a["src"], ATOMS),
        "src_rows": np.ascontiguousarray(by_tile(a["src"], ATOMS)),
        "dst_cols": cols(a["dst"], 0),
        "attr_t": np.ascontiguousarray(by_tile(a["edge_attr_64"], 0).reshape(PAD_EDGES, R).T),
        "weight_cols": cols(a["edge_weight1"][:, 0], 0),
        "w_in": a["L0_gnn_W_in2f"], "wf1": a["L0_gnn_Wf1"], "bf1": chunked(a["L0_gnn_bf1"]),
        "wf2": a["L0_gnn_Wf2"], "bf2": chunked(a["L0_gnn_bf2"]), "wo1": a["L0_gnn_Wo1"],
        "bo1": chunked(a["L0_gnn_bo1"]), "wo2": a["L0_gnn_Wo2"], "bo2": a["L0_gnn_bo2"].reshape(1, F),
    }
    feeds = {f"in_{k}": np.ascontiguousarray(v) for k, v in arrays.items()}
    args = [nc.dram_tensor(k, v.shape, mb.dt.from_np(v.dtype), kind="ExternalInput").ap() for k, v in feeds.items()]
    out = nc.dram_tensor("out_rows", (OUT_ROWS, F), mb.dt.float32, kind="ExternalOutput").ap()
    build(nc, *args, out)
    r = run(nc, [feeds], core_ids=[0])
    return r.results[0]["out_rows"][:ATOMS]
```

```python
import math
from contextlib import ExitStack

import concourse.bass as bass
from concourse import mybir

P = 128
ATOMS, EDGES, F, R = 100000, 25000, 256, 64
KC = F // P
JT = 4
QE = JT * P
QUADS = -(-EDGES // QE)
TILES = QUADS * JT
PAD_EDGES = QUADS * QE
GA = 8
GR = GA * P
GROUPS = -(-ATOMS // GR)
OVERLAP = GROUPS * GR - ATOMS
RING = 20
WRITE_QUADS = 3
EARLY = 20
E2 = EARLY // 2
FAST = 44
FAST_FROM = 3 * (FAST // 2 - E2)
AFTER = FAST_FROM + 2 * (QUADS - FAST)
TABLE_TRASH = -(-(ATOMS + 1) // P) * P
TABLE_ROWS = TABLE_TRASH + QE
SUM_TRASH = PAD_EDGES
ZERO_A = 12
ZERO_QUADS = EARLY - 2
SUM_ROWS = ZERO_QUADS * ZERO_A * P
OUT_TRASH = TABLE_TRASH
OUT_ROWS = OUT_TRASH + 2 * QE
LOG2 = math.log(2.0)
EPS = 1e-5
EXP_CAP = 2.0 ** 60
assert GROUPS == 2 * QUADS and SUM_ROWS >= SUM_TRASH + QE and ZERO_QUADS <= EARLY
assert QUADS == 5 * (E2 - 1) + 4 and EARLY <= RING and AFTER == QUADS - 3 and QUADS % 2 == 1


def build(nc, x, src_cols, src_rows, dst_cols, attr_t, weight_cols, w_in, wf1, bf1, wf2, bf2, wo1, bo1, wo2, bo2, out):
    f32, i32, bf16 = mybir.dt.float32, mybir.dt.int32, mybir.dt.bfloat16
    ALU, ACT = mybir.AluOpType, mybir.ActivationFunctionType
    ctx = ExitStack()
    with ctx:
        def sb(name, shape, dt=f32):
            return ctx.enter_context(nc.sbuf_tensor(name, shape, dt))

        def ps(name):
            return ctx.enter_context(nc.psum_tensor(name, [P, KC, QE], f32))

        def sem(name):
            return ctx.enter_context(nc.semaphore(name))

        def sems(name, n):
            return [sem(f"{name}{i}") for i in range(n)]

        table = nc.dram_tensor("rep_table", (TABLE_ROWS, 1), i32, kind="Internal").ap()
        sums = nc.dram_tensor("segment_sums", (SUM_ROWS, F), f32, kind="Internal").ap()

        xs = sb("xs", [P, 4, GA, F])
        hs = sb("hs", [P, 2, GA, F])
        ring = sb("ring", [P, RING, JT, F])
        row_now = sb("row_now", [P, 3, JT, F])
        row_flat = row_now[:, :, :, :].rearrange("p k j f -> p (k j f)")
        MATCHES = JT * (JT + 1) // 2 * P
        pre_row = row_flat[:, 0:WRITE_QUADS * QE].bitcast(i32).rearrange("p (k e) -> p k e", k=WRITE_QUADS)
        hits = row_flat[:, WRITE_QUADS * QE:WRITE_QUADS * QE + MATCHES].bitcast(bf16).rearrange(
            "p (k e) -> p k e", k=2)
        xg = sb("xg", [P, 2, JT, F])
        h_rows = sb("h_rows", [P, JT, F])
        attr = sb("attr", [R, 2, QE])
        src_row = sb("src_row", [P, 2, QE], i32)
        h_t = sb("h_t", [P, KC, QE])
        soft = sb("soft", [P, KC, QE])
        msg = sb("msg", [P, KC, QE])
        y_rows = sb("y_rows", [P, JT, F])
        same = sb("same", [P, MATCHES])
        same_at = [j * (j + 1) // 2 * P for j in range(JT)]
        w_in_s = sb("w_in_s", [P, KC, F])
        wf1_s = sb("wf1_s", [R, F])
        wf2_s = sb("wf2_s", [P, KC, F])
        wo1_s = sb("wo1_s", [P, KC, F])
        wo2_s = sb("wo2_s", [P, KC, F])
        bf1_c = sb("bf1_c", [P, KC])
        bf2_c = sb("bf2_c", [P, KC])
        bo1_c = sb("bo1_c", [P, KC])
        filt_bias = sb("filt_bias", [P, KC])
        sp0 = sb("sp0", [P, KC])
        sp0_shift = sb("sp0_shift", [P, KC])
        lean_row = sb("lean_row", [P, F])
        lone_row = sb("lone_row", [P, F])
        bo2_row = y_rows[:, 2]
        lone_hi, lone_mid = hits[:, 0, 0:F], hits[:, 0, F:2 * F]
        lone_rest, lone_low = msg[:, 0, 0:F], msg[:, 0, F:2 * F]
        lone_sum = msg[:, 1, 0:F]
        ident = sb("ident", [P, P])
        earlier = sb("earlier", [P, JT, P], bf16)
        all_ones = sb("all_ones", [P, P], bf16)
        lone_parts = sb("lone_parts", [P, 2, F], bf16)
        ones = y_rows[:, 3, 0:P]
        zeros = sb("zeros", [P, F])
        neg_log2 = sb("neg_log2", [P, 1])
        eps_col = sb("eps_col", [P, 1])
        src_i = sb("src_i", [P, TILES], i32)
        dst_i = sb("dst_i", [P, TILES], i32)
        src_f = sb("src_f", [P, TILES])
        weight = sb("weight", [P, TILES])
        edge_i = sb("edge_i", [P, TILES], i32)
        trash_i = sb("trash_i", [P, JT * 2], i32)
        table_idx = sb("table_idx", [P, TILES], i32)
        spare_table = sb("spare_table", [P, TILES], i32)
        spare_less_src = sb("spare_less_src", [P, TILES])
        spare_sum = sb("spare_sum", [P, TILES], i32)
        rep_i = sb("rep_i", [P, TILES], i32)
        out_idx = spare_table
        dst_now = sb("dst_now", [P, 2, JT], i32)
        idx_now = sb("idx_now", [P, 2, WRITE_QUADS * JT], i32)
        val_now = sb("val_now", [P, 2, WRITE_QUADS * JT], i32)
        cover = sb("cover", [P, WRITE_QUADS * JT])
        idx_add = sb("idx_add", [P, WRITE_QUADS * JT])
        val_add = sb("val_add", [P, WRITE_QUADS * JT])
        look_idx = sb("look_idx", [P, 3, JT], i32)
        rep_now = sb("rep_now", [P, 3, JT], i32)
        NS = 2 * GA + JT
        stats = sb("stats", [P, 2, NS, 6])
        st_a = sb("st_a", [P, NS])
        st_b = sb("st_b", [P, NS])
        st_c = sb("st_c", [P, NS])
        st_sum = sb("st_sum", [P, NS])
        st_var = sb("st_var", [P, NS])
        st_ln = sb("st_ln", [P, NS])
        st_seed = sb("st_seed", [P, NS])
        rstd = sb("rstd", [P, 2, NS])
        shift = sb("shift", [P, 2, NS])

        ps_a = ps("ps_a")
        ps_f = ps("ps_f")
        ps_h = ps("ps_h")
        ps_u = ps("ps_u")

        weights_in = sems("weights_in", 15)
        x_loaded = sems("x_loaded", 4)
        out_stored = sems("out_stored", 2)
        attr_loaded = sems("attr_loaded", 2)
        row_loaded = sems("row_loaded", 2)
        pre_loaded = sems("pre_loaded", 3)
        pre_used = sem("pre_used")
        sums_zeroed = sem("sums_zeroed")
        trash_zeroed = sem("trash_zeroed")
        const_made = sem("const_made")
        zero_made = sem("zero_made")
        iota_made = sem("iota_made")
        ident_step = sem("ident_step")
        src_f_made = sem("src_f_made")
        index_step = sem("index_step")
        spare_made = sem("spare_made")
        setup_dve = sem("setup_dve")
        setup_act = sem("setup_act")
        setup_pe = sem("setup_pe")
        setup_done = sem("setup_done")
        lone_step = sem("lone_step")
        table_written = sem("table_written")
        looked = sems("looked", 3)
        gathered = sems("gathered", 2)
        pool_waits = sem("pool_waits")
        staged = sem("staged")
        rep_saved = sem("rep_saved")
        rows_staged = sem("rows_staged")
        added = sem("added")
        stats_made = sem("stats_made")
        small_step = sem("small_step")
        var_ready = sem("var_ready")
        ln_var = sem("ln_var")
        seed_ready = sem("seed_ready")
        norm_ready = sem("norm_ready")
        edges_normed = sem("edges_normed")
        stream_normed = sem("stream_normed")
        x_copied = sem("x_copied")
        x_added = sem("x_added")
        half_summed = sem("half_summed")
        filt1_done = sem("filt1_done")
        exp_done = sem("exp_done")
        capped = sem("capped")
        log_done = sem("log_done")
        soft_ready = sem("soft_ready")
        transposed = sem("transposed")
        h_t_ready = sem("h_t_ready")
        proj_done = sem("proj_done")
        proj_ready = sem("proj_ready")
        filt2_done = sem("filt2_done")
        msg_ready = sem("msg_ready")
        y_done = sem("y_done")
        y_ready = sem("y_ready")
        same_ready = sem("same_ready")
        merged = sem("merged")
        rows_ready = sem("rows_ready")
        sum_loaded = sems("sum_loaded", 2)
        f_transposed = sem("f_transposed")
        f_exp = sem("f_exp")
        f_capped = sem("f_capped")
        f_log = sem("f_log")
        f_soft = sem("f_soft")
        f_out = sem("f_out")
        f_rows = sem("f_rows")
        out_idx_step = sem("out_idx_step")
        out_idx_made = sem("out_idx_made")
        out_added = sems("out_added", 2)

        block = ctx.enter_context(nc.Block())

        def flat(t):
            return t.rearrange("p a b -> p (a b)")

        def group_rows(dram, base):
            return dram[bass.ds(base, GR), :].rearrange("(p a) f -> p a f", a=GA)

        def group_base(g):
            return 0 if isinstance(g, int) and g == 0 else g * GR - OVERLAP

        @block.sync
        def _(sp):
            def load(n, dst, source):
                sp.dma_start(dst, source).then_inc(weights_in[n], 16)

            def row_of(q):
                return src_rows[bass.ds(q, 1), :].partition_broadcast(P)

            def load_pre(n, k):
                sp.dma_start(pre_row[:, k], row_of(n)).then_inc(pre_loaded[k], 16)

            def by_chunk(w):
                return w.rearrange("(k p) f -> p k f", p=P)

            load(0, src_i[:, :], src_cols)
            load(1, dst_i[:, :], dst_cols)
            for k in range(WRITE_QUADS):
                load_pre(k, k)
            load(10, bo1_c[:, :], bo1)
            load(9, bf2_c[:, :], bf2)
            load(11, bo2_row[:, :], bo2.partition_broadcast(P))
            load(5, wf2_s[:, :, :], by_chunk(wf2))
            load(7, wo2_s[:, :, :], by_chunk(wo2))
            for g in range(2):
                sp.dma_start(xs[:, g], group_rows(x, group_base(g))).then_inc(x_loaded[g], 16)
            load(8, bf1_c[:, :], bf1)
            load(3, wf1_s[:, :], wf1)
            for q in range(2):
                sp.dma_start(attr[:, q], attr_t[:, bass.ts(q, QE)]).then_inc(attr_loaded[q], 16)
                sp.dma_start(src_row[:, q], row_of(q)).then_inc(row_loaded[q], 16)
            load(2, weight[:, :], weight_cols)
            load(4, w_in_s[:, :, :], by_chunk(w_in))
            load(6, wo1_s[:, :, :], by_chunk(wo1))
            for g in range(2, 4):
                sp.dma_start(xs[:, g], group_rows(x, group_base(g))).then_inc(x_loaded[g], 16)
            sp.wait_ge(zero_made, 1)

            def body(q, s, zero=False, pre=()):
                static = isinstance(q, int)
                if zero:
                    sp.dma_start(sums[bass.ds(q * (ZERO_A * P), ZERO_A * P), :].rearrange("(p a) f -> p a f", a=ZERO_A),
                                 zeros[:, :].unsqueeze(1).broadcast_to([P, ZERO_A, F])).then_inc(sums_zeroed, 16)
                for h in range(2):
                    sp.wait_ge(half_summed, q * 4 + 2 * h + 2)
                    if static and q == 0 and h == 1:
                        sp.wait_ge(out_stored[0], 16)
                    sp.dma_start(group_rows(out, group_base(q * 2 + h)), hs[:, h]).then_inc(out_stored[h], 16)
                    if not static or q < QUADS - 2:
                        sp.dma_start(xs[:, 2 * s + h], group_rows(x, group_base(q * 2 + h + 4))
                                     ).then_inc(x_loaded[2 * s + h], 16)
                    if h == 0:
                        if not static or q < QUADS - 2:
                            sp.wait_ge(filt1_done, q + 1)
                            sp.dma_start(attr[:, s], attr_t[:, bass.ds((q + 2) * QE, QE)]).then_inc(attr_loaded[s], 16)
                        if not static or 0 < q < QUADS - 1:
                            sp.wait_ge(same_ready, q)
                            sp.dma_start(src_row[:, 1 - s], row_of(q + 1)).then_inc(row_loaded[1 - s], 16)
                        for k, (n, used) in enumerate(pre):
                            sp.wait_ge(pre_used, used)
                            load_pre(n, k)

            for k in range(2):
                sp.wait_ge(pre_used, k + 1)
                load_pre(WRITE_QUADS + k, k)

            def pre_even(r):
                return (r * 5 + 5, r * 5 + 4), (r * 5 + 6, r * 5 + 5), (r * 5 + 7, r * 5 + 3)

            def pre_odd(r):
                return (r * 5 + 8, r * 5 + 6), (r * 5 + 9, r * 5 + 7)

            body(0, 0, True, pre_even(0))
            body(1, 1, True, pre_odd(0))
            sp.dma_start(out[ATOMS:OUT_ROWS, :].rearrange("(p a) f -> p a f", a=(OUT_ROWS - ATOMS) // 112),
                         zeros[0:112, :].unsqueeze(1).broadcast_to([112, (OUT_ROWS - ATOMS) // 112, F])
                         ).then_inc(trash_zeroed, 16)
            with sp.Fori(1, E2 - 2) as r:
                body(r * 2, 0, True, pre_even(r))
                body(r * 2 + 1, 1, True, pre_odd(r))
            body(16, 0, True, pre_even(8)[:2])
            body(17, 1, True, ((47, 46), (48, 47)))
            with sp.Fori(E2 - 1, 23) as r:
                body(r * 2, 0)
                body(r * 2 + 1, 1)
            body(46, 0)
            body(47, 1)
            body(48, 0)

            sp.wait_ge(added, 16 * TILES)

            def load_sums(q, s, wait=True):
                if wait:
                    sp.wait_ge(f_transposed, q - 1)
                sp.dma_start(ring[:, s], sums[bass.ds(q * QE, QE), :].rearrange("(p j) f -> p j f", j=JT)
                             ).then_inc(sum_loaded[s], 16)

            load_sums(0, 0, False)
            load_sums(1, 1, False)
            with sp.Fori(1, QUADS // 2) as r:
                load_sums(r * 2, 0)
                load_sums(r * 2 + 1, 1)
            load_sums(QUADS - 1, 0)

        @block.gpsimd
        def _(pool):
            pool.memset(all_ones[:, :], 1.0).then_inc(ident_step, 1)
            pool.memset(ident[:, :], 0.0).then_inc(ident_step, 1)
            pool.memset(earlier[:, :, :], 1.0).then_inc(ident_step, 1)
            pool.iota(edge_i[:, :], [[QE, QUADS], [1, JT]], base=0, channel_multiplier=JT).then_inc(iota_made, 1)
            pool.iota(trash_i[:, :], [[P, 2 * JT]], base=OUT_TRASH, channel_multiplier=1).then_inc(iota_made, 1)
            pool.iota(spare_table[:, :], [[0, QUADS], [P, JT]], base=TABLE_TRASH, channel_multiplier=1).then_inc(iota_made, 1)
            pool.iota(spare_sum[:, :], [[-QE, QUADS], [P - 1, JT]], base=SUM_TRASH, channel_multiplier=1 - JT
                      ).then_inc(iota_made, 1)
            pool.wait_ge(ident_step, 3)
            pool.affine_select(out=ident[:, :], in_=ident[:, :], compare_op=ALU.not_equal, fill=1.0, base=0,
                               pattern=[[-1, P]], channel_multiplier=1).then_inc(const_made, 1)
            last = earlier[:, JT - 1, :]
            pool.affine_select(out=last, in_=last, compare_op=ALU.is_gt, fill=0.0, base=0,
                               pattern=[[-1, P]], channel_multiplier=1).then_inc(const_made, 1)

            def at(idx):
                return bass.IndirectOffsetOnAxis(ap=idx, axis=0)

            def wait_alone(sem, value):
                pool.wait_ge(sem, value)
                pool.sem_inc(pool_waits, 1)

            def gather(idx, s, j):
                pool.indirect_dma_start(xg[:, s, j], None, x[:, :], at(idx)).then_inc(gathered[s], 16)

            def write_table(n, s, k):
                if not (isinstance(n, int) and n == 0):
                    wait_alone(table_written, n * (16 * JT))
                for j in range(JT):
                    c = k * JT + j
                    pool.indirect_dma_start(table[:, :], at(idx_now[:, s, c:c + 1]), val_now[:, s, c:c + 1], None
                                            ).then_inc(table_written, 16)

            def look(idx, k):
                for j in range(JT):
                    pool.indirect_dma_start(rep_now[:, k, j:j + 1], None, table[:, :], at(idx[:, j:j + 1])
                                            ).then_inc(looked[k], 16)

            def look_again(n, k):
                wait_alone(rep_saved, n - 2)
                look(look_idx[:, k], k)

            def add_rows(n, k, times):
                if not (isinstance(n, int) and n == 0):
                    wait_alone(added, n * (16 * JT))
                wait_alone(looked[k], times * (16 * JT))
                wait_alone(rows_staged, n + 1)
                for j in range(JT):
                    pool.indirect_dma_start(sums[:, :], at(rep_now[:, k, j:j + 1]), row_now[:, k, j], None,
                                            compute_op=ALU.add).then_inc(added, 16)

            def gather_pair(q, s, b):
                if b == 0:
                    wait_alone(edges_normed, q + 1)
                for j in (2 * b, 2 * b + 1):
                    gather(dst_now[:, s, j:j + 1], s, j)

            pool.wait_ge(weights_in[1], 16)
            for q in range(2):
                for j in range(JT):
                    gather(dst_i[:, q * JT + j:q * JT + j + 1], q, j)

            def early(q, s, n, count=WRITE_QUADS):
                wait_alone(staged, q + 1)
                write_table(n, s, 0)
                gather_pair(q, s, 0)
                write_table(n + 1, s, 1)
                gather_pair(q, s, 1)
                if count == 3:
                    write_table(n + 2, s, 2)

            early(0, 0, 0)
            early(1, 1, 3, 2)
            with pool.Fori(1, E2 - 1) as r:
                early(r * 2, 0, r * 5)
                early(r * 2 + 1, 1, r * 5 + 3, 2)
            early(18, 0, 45, 2)
            early(19, 1, 47, 2)

            pool.wait_ge(staged, EARLY + 1)
            gather_pair(EARLY, 0, 0)
            gather_pair(EARLY, 0, 1)
            pool.wait_ge(table_written, 16 * TILES)
            for k in range(3):
                look(table_idx[:, k * JT:(k + 1) * JT], k)
            pool.wait_ge(sums_zeroed, 16 * ZERO_QUADS)
            add_rows(0, 0, 1)

            def unit(n, k, times, more=True):
                add_rows(n, k, times)
                if more:
                    look_again(n + 2, (k + 2) % 3)

            def fetch(q, s):
                wait_alone(staged, q + 1)
                gather_pair(q, s, 0)
                gather_pair(q, s, 1)

            fetch(21, 1)
            unit(1, 1, 1)
            unit(2, 2, 1)
            with pool.Fori(E2 + 1, FAST // 2) as r:
                fetch(r * 2, 0)
                unit((r - E2) * 3, 0, r - E2 + 1)
                fetch(r * 2 + 1, 1)
                unit((r - E2) * 3 + 1, 1, r - E2 + 1)
                unit((r - E2) * 3 + 2, 2, r - E2 + 1)
            for n in range(FAST_FROM, QUADS):
                q = FAST + (n - FAST_FROM) // 2
                if (n - FAST_FROM) % 2 == 0 and q < QUADS - 2:
                    fetch(q, q % 2)
                unit(n, n % 3, n // 3 + 1, n < QUADS - 2)

            pool.wait_ge(out_idx_made, 1)
            for h in range(2):
                pool.wait_ge(out_stored[h], 16 * QUADS)
            pool.wait_ge(trash_zeroed, 16)

            def add_out(q, s, wait=True):
                wait_alone(f_rows, q + 1)
                if wait:
                    wait_alone(out_added[s], (q - s) * 32)
                for j in range(JT):
                    pool.indirect_dma_start(out[:, :], at(dst_now[:, s, j:j + 1]), ring[:, 4 + s, j], None,
                                            compute_op=ALU.add).then_inc(out_added[s], 16)

            add_out(0, 0, False)
            add_out(1, 1, False)
            with pool.Fori(1, QUADS // 2) as r:
                add_out(r * 2, 0)
                add_out(r * 2 + 1, 1)
            add_out(QUADS - 1, 0)
            pool.wait_ge(out_added[0], 64 * (QUADS // 2 + 1))
            pool.wait_ge(out_added[1], 64 * (QUADS // 2))

        @block.scalar
        def _(act):
            act.preload_act_table_set("natural_log_exp_and_others")
            act.wait_ge(weights_in[10], 16)
            act.activation(sp0[:, :], bo1_c[:, :], ACT.Exp).then_inc(setup_act, 1)
            act.wait_ge(setup_dve, 2)
            act.activation(sp0[:, :], sp0[:, :], ACT.Ln, bias=1.0).then_inc(setup_act, 1)

            def seed(n):
                act.wait_ge(var_ready, n)
                act.activation(st_ln[:, :], st_var[:, :], ACT.Ln, bias=eps_col[:, :]).then_inc(ln_var, 1)
                act.wait_ge(ln_var, n)
                act.activation(st_seed[:, :], st_ln[:, :], ACT.Exp, scale=-0.5).then_inc(seed_ready, 1)

            seed(1)

            def stage_rows(n, k):
                act.wait_ge(rows_ready, n + 1)
                if not (isinstance(n, int) and n < 3):
                    act.wait_ge(added, (n - 2) * (16 * JT))
                act.activation(row_now[:, k], ring[:, bass.ds(n % RING, 1)].squeeze(1), ACT.Copy
                               ).then_inc(rows_staged, 1)

            def keep_rows(q, slot):
                act.wait_ge(merged, q + 1)
                dst = ring[:, bass.ds(slot, 1)].rearrange("p o j f -> p (o j f)")
                for k in range(KC):
                    ins = act.activation(dst[:, bass.ts(k, QE)], ps_f[:, k], ACT.Copy)
                ins.then_inc(rows_ready, 1)

            def copy_y(q):
                act.wait_ge(y_done, q + 1)
                if not (isinstance(q, int) and q == 0):
                    act.wait_ge(merged, q)
                y_flat = flat(y_rows[:, :, :])
                for k in range(KC):
                    ins = act.activation(y_flat[:, bass.ts(k, QE)], ps_h[:, k], ACT.Copy)
                ins.then_inc(y_ready, 1)

            def copy_proj(q):
                act.wait_ge(proj_done, q + 1)
                if not (isinstance(q, int) and q == 0):
                    act.wait_ge(y_done, q)
                for k in range(KC):
                    ins = act.activation(msg[:, k], ps_h[:, k], ACT.Copy)
                ins.then_inc(proj_ready, 1)

            def body(q, s, slot=None, stage=(), last=False):
                static = isinstance(q, int)

                def norm_stream(half):
                    h, a0 = half // 2, (half % 2) * 4
                    if half % 2 == 0 and not (static and q == 0):
                        act.wait_ge(out_stored[h], q * 16)
                    for a in range(a0, a0 + 4):
                        c = h * GA + a
                        ins = act.activation(hs[:, h, a], xs[:, 2 * s + h, a], ACT.Relu,
                                             bias=shift[:, s, c:c + 1], scale=rstd[:, s, c:c + 1])
                    ins.then_inc(stream_normed, 1)

                if not static or q > 1:
                    keep_rows(q - 2, slot)
                act.wait_ge(norm_ready, q + 1)
                if not (static and q == 0):
                    act.wait_ge(transposed, q)
                for j in range(JT):
                    c = 2 * GA + j
                    ins = act.activation(h_rows[:, j], xg[:, s, j], ACT.Relu,
                                         bias=shift[:, s, c:c + 1], scale=rstd[:, s, c:c + 1])
                ins.then_inc(edges_normed, 1)
                norm_stream(0)
                if not (static and q == 0):
                    copy_proj(q - 1)
                norm_stream(1)
                for n, k in stage:
                    stage_rows(n, k)
                act.wait_ge(filt1_done, q + 1)
                if not (static and q == 0):
                    act.wait_ge(filt2_done, q)
                for k in range(KC):
                    ins = act.activation(soft[:, k], ps_a[:, k], ACT.Exp, bias=bf1_c[:, k:k + 1])
                ins.then_inc(exp_done, 1)
                norm_stream(2)
                act.wait_ge(capped, q + 1)
                act.activation(flat(soft[:, :, :]), flat(soft[:, :, :]), ACT.Ln, bias=1.0).then_inc(log_done, 1)
                if not (static and q == 0):
                    copy_y(q - 1)
                norm_stream(3)
                act.wait_ge(transposed, q + 1)
                if not (static and q == 0):
                    act.wait_ge(proj_done, q)
                for k in range(KC):
                    ins = act.activation(h_t[:, k], ps_h[:, k], ACT.Copy)
                ins.then_inc(h_t_ready, 1)
                if not last:
                    seed(q + 2)

            body(0, 0)
            body(1, 1)
            with act.Fori(1, E2) as r:
                body(r * 2, 0, r * 2 - 2)
                body(r * 2 + 1, 1, r * 2 - 1)
            body(20, 0, 18, ((0, 0),))
            body(21, 1, 19, ((1, 1), (2, 2)))
            with act.Fori(E2 + 1, FAST // 2) as r:
                body(r * 2, 0, (r * 2 - 2) % RING, (((r - E2) * 3, 0),))
                body(r * 2 + 1, 1, (r * 2 - 1) % RING, (((r - E2) * 3 + 1, 1), ((r - E2) * 3 + 2, 2)))
            for q in range(FAST, QUADS):
                n = (q - FAST) * 2 + FAST_FROM
                body(q, q % 2, (q - 2) % RING, ((n, n % 3), (n + 1, (n + 1) % 3)), last=(q == QUADS - 1))
            end = QUADS - 1
            keep_rows(end - 1, (end - 1) % RING)
            copy_proj(end)
            stage_rows(end - 2, (end - 2) % 3)
            copy_y(end)
            stage_rows(end - 1, (end - 1) % 3)
            keep_rows(end, end % RING)
            stage_rows(end, end % 3)

            def f_first(q, s, wait=True):
                act.wait_ge(f_transposed, q + 1)
                if wait:
                    act.wait_ge(f_soft, q - 1)
                for k in range(KC):
                    ins = act.activation(flat(ring[:, 2 + s])[:, bass.ts(k, QE)], (ps_f, ps_h)[s][:, k], ACT.Exp,
                                         bias=bo1_c[:, k:k + 1])
                ins.then_inc(f_exp, 1)

            def f_second(q, s):
                act.wait_ge(f_capped, q + 1)
                act.activation(flat(ring[:, 2 + s]), flat(ring[:, 2 + s]), ACT.Ln, bias=1.0).then_inc(f_log, 1)

            f_first(0, 0, False)
            f_first(1, 1, False)
            f_second(0, 0)
            f_second(1, 1)
            with act.Fori(1, QUADS // 2) as r:
                f_first(r * 2, 0)
                f_second(r * 2, 0)
                f_first(r * 2 + 1, 1)
                f_second(r * 2 + 1, 1)
            f_first(QUADS - 1, 0)
            f_second(QUADS - 1, 0)

        @block.tensor
        def _(pe):
            pe.wait_ge(const_made, 2)
            pe.wait_ge(weights_in[5], 16)
            pe.wait_ge(setup_dve, 1)
            for c in range(KC):
                for k in range(KC):
                    ins = pe.matmul(ps_f[:, 0, c:c + 1], wf2_s[:, k, bass.ts(c, P)], neg_log2[:, :],
                                    start=(k == 0), stop=(k == KC - 1))
            ins.then_inc(setup_pe, 1)
            pe.wait_ge(setup_dve, 6)
            pe.wait_ge(weights_in[7], 16)
            for v in range(2):
                for k in range(KC):
                    ins = pe.matmul(ps_h[:, v, 0:F], y_rows[:, k, v * P:(v + 1) * P], wo2_s[:, k],
                                    start=(k == 0), stop=(k == KC - 1))
            ins.then_inc(setup_pe, 1)
            pe.wait_ge(lone_step, 6)
            for n in (3, 4, 6):
                pe.wait_ge(weights_in[n], 16)

            def copy_x(q, s, b, before):
                h, a0 = b // 2, (b % 2) * 4
                if b % 2 == 0:
                    pe.wait_ge(x_loaded[2 * s + h], q * 8 + (16 if s == 0 else 8))
                if not (isinstance(q, int) and q * 4 + before <= 0):
                    pe.wait_ge(half_summed, q * 4 + before)
                for k in range(2):
                    pe.matmul(ps_u[:, k], ident[:, :], xs[:, 2 * s + h, a0 + 2 * k:a0 + 2 * k + 2]
                              .rearrange("p a f -> p (a f)"), start=True, stop=False)
                    ins = pe.matmul(ps_u[:, k], all_ones[:, :], flat(lone_parts[:, :, :]), start=False, stop=True)
                ins.then_inc(x_copied, 1)

            def body(q, s, copies=((), (), ()), front=True, back=True):
                if back:
                    pe.wait_ge(h_t_ready, q)
                    for c in range(KC):
                        for k in range(KC):
                            ins = pe.matmul(ps_h[:, c], w_in_s[:, k, bass.ts(c, P)], h_t[:, k],
                                            start=(k == 0), stop=(k == KC - 1))
                    ins.then_inc(proj_done, 1)
                for b, before in copies[0]:
                    copy_x(q, s, b, before)
                if back:
                    pe.wait_ge(soft_ready, q)
                    if not (isinstance(q, int) and q == 1):
                        pe.wait_ge(rows_ready, q - 1)
                    for c in range(KC):
                        for k in range(KC):
                            ins = pe.matmul(ps_f[:, c], wf2_s[:, k, bass.ts(c, P)], soft[:, k],
                                            start=(k == 0), stop=(k == KC - 1))
                    ins.then_inc(filt2_done, 1)
                if front:
                    pe.wait_ge(attr_loaded[s], q * 8 + (16 if s == 0 else 8))
                    for c in range(KC):
                        ins = pe.matmul(ps_a[:, c], wf1_s[:, bass.ts(c, P)], attr[:, s], start=True, stop=True)
                    ins.then_inc(filt1_done, 1)
                for b, before in copies[1]:
                    copy_x(q, s, b, before)
                if back:
                    pe.wait_ge(msg_ready, q)
                    rows = ps_h[:, :, :].rearrange("p k (a f) -> p (k a) f", f=F)
                    for j in range(JT):
                        for k in range(KC):
                            ins = pe.matmul(rows[:, j], msg[:, k, bass.ts(j, P)], wo1_s[:, k],
                                            start=(k == 0), stop=(k == KC - 1))
                    ins.then_inc(y_done, 1)
                for b, before in copies[2]:
                    copy_x(q, s, b, before)
                if back:
                    pe.wait_ge(y_ready, q)
                if front:
                    pe.wait_ge(edges_normed, q + 1)
                    for k in range(KC):
                        for j in range(JT):
                            ins = pe.transpose(ps_h[:, k, bass.ts(j, P)], h_rows[:, j, bass.ts(k, P)], ident[:, :])
                    ins.then_inc(transposed, 1)
                if back:
                    pe.wait_ge(same_ready, q)
                    rows = ps_f[:, :, :].rearrange("p k (a f) -> p (k a) f", f=F)
                    for i in range(JT):
                        for j in range(i, JT):
                            ins = pe.matmul(rows[:, i], same[:, same_at[j] + i * P:same_at[j] + (i + 1) * P], y_rows[:, j],
                                            start=(j == i), stop=(j == JT - 1))
                    ins.then_inc(merged, 1)

            early = ((0, -1),), ((1, 1),), ((2, 2),)
            body(0, 0, early, back=False)
            body(1, 1, early)
            with pe.Fori(1, E2) as r:
                body(r * 2, 0, early)
                body(r * 2 + 1, 1, early)
            with pe.Fori(E2, QUADS // 2) as r:
                body(r * 2, 0, ((), (), ((2, -1),)))
                body(r * 2 + 1, 1, ((), ((1, -1),), ((2, 2),)))
            body(QUADS - 1, 0, ((), (), ((2, -1),)))
            body(QUADS, 1, front=False)

            def f_turn(q, s, wait=True):
                pe.wait_ge(sum_loaded[s], q * 8 + (16 if s == 0 else 8))
                if wait:
                    pe.wait_ge(f_soft, q - 1)
                for k in range(KC):
                    for j in range(JT):
                        ins = pe.transpose((ps_f, ps_h)[s][:, k, bass.ts(j, P)], ring[:, s, j, bass.ts(k, P)], ident[:, :])
                ins.then_inc(f_transposed, 1)

            def f_mul(q, s, wait=True):
                pe.wait_ge(f_soft, q + 1)
                if wait:
                    pe.wait_ge(f_rows, q - 1)
                sp_t = flat(ring[:, 6 + s]).rearrange("p (k e) -> p k e", k=KC)
                rows = (ps_a, ps_u)[s][:, :, :].rearrange("p k (a f) -> p (k a) f", f=F)
                for j in range(JT):
                    for k in range(KC):
                        ins = pe.matmul(rows[:, j], sp_t[:, k, bass.ts(j, P)], wo2_s[:, k],
                                        start=(k == 0), stop=(k == KC - 1))
                ins.then_inc(f_out, 1)

            pe.wait_ge(rows_ready, QUADS)
            f_turn(0, 0, False)
            f_turn(1, 1, False)
            f_turn(2, 0)
            f_mul(0, 0, False)
            f_turn(3, 1)
            f_mul(1, 1, False)
            with pe.Fori(2, QUADS // 2) as r:
                f_turn(r * 2, 0)
                f_mul(r * 2 - 2, 0)
                f_turn(r * 2 + 1, 1)
                f_mul(r * 2 - 1, 1)
            f_turn(QUADS - 1, 0)
            f_mul(QUADS - 3, 0)
            f_mul(QUADS - 2, 1)
            f_mul(QUADS - 1, 0)

        @block.vector
        def _(dve):
            dve.memset(eps_col[:, :], EPS)
            dve.memset(neg_log2[:, :], -LOG2).then_inc(setup_dve, 1)
            dve.memset(ones[:, :], 1.0)
            dve.memset(zeros[:, :], 0.0).then_inc(zero_made, 1)
            dve.wait_ge(weights_in[0], 16)
            dve.tensor_copy(src_f[:, :], src_i[:, :]).then_inc(src_f_made, 1)
            dve.wait_ge(src_f_made, 1)
            dve.wait_ge(iota_made, 4)
            dve.tensor_tensor(spare_less_src[:, :], spare_table[:, :], src_f[:, :], ALU.subtract).then_inc(spare_made, 1)
            dve.wait_ge(spare_made, 1)
            dve.wait_ge(const_made, 2)
            dve.wait_ge(weights_in[1], 16)

            def cover_quad(n, k, wait, loads):
                dve.wait_ge(pre_loaded[k], loads * 16)
                if wait:
                    dve.wait_ge(pre_used, n if k == 0 else n - 1)
                at = 0
                for j in range(JT):
                    w = (j + 1) * P
                    ins = dve.scalar_tensor_tensor(out=hits[:, k % 2, at:at + w], in0=pre_row[:, k, 0:w],
                                                   scalar=src_f[:, bass.ds(n * JT + j, 1)],
                                                   in1=earlier[:, JT - 1 - j:JT].rearrange("p a i -> p (a i)"),
                                                   op0=ALU.is_equal, op1=ALU.mult,
                                                   accum_out=cover[:, k * JT + j:k * JT + j + 1])
                    at += w
                ins.then_inc(pre_used, 1)

            def plan(q, s, n, count, written):
                w = count * JT
                cols = bass.ds(n * JT, w)
                dve.wait_ge(pre_used, n + count)
                dve.scalar_tensor_tensor(out=idx_add[:, 0:w], in0=cover[:, 0:w], scalar=1.0, in1=spare_less_src[:, cols],
                                         op0=ALU.min, op1=ALU.mult).then_inc(index_step, 1)
                dve.scalar_tensor_tensor(out=val_add[:, 0:w], in0=cover[:, 0:w], scalar=1.0, in1=spare_sum[:, cols],
                                         op0=ALU.min, op1=ALU.mult).then_inc(index_step, 1)
                if not (isinstance(q, int) and q < 2):
                    dve.wait_ge(table_written, written * (16 * JT))
                dve.wait_ge(index_step, q * 3 + 1)
                dve.tensor_tensor(idx_now[:, s, 0:w], idx_add[:, 0:w], src_f[:, cols], ALU.add).then_inc(index_step, 1)
                dve.wait_ge(index_step, q * 3 + 2)
                dve.tensor_tensor(val_now[:, s, 0:w], val_add[:, 0:w], edge_i[:, cols], ALU.add)
                dve.wait_ge(index_step, q * 3 + 3)
                dve.tensor_copy(table_idx[:, cols], idx_now[:, s, 0:w]).then_inc(staged, 1)

            def stage_dst(q, s):
                return dve.tensor_copy(dst_now[:, s], dst_i[:, bass.ds((q + 2) * JT, JT)])

            for k in range(WRITE_QUADS):
                cover_quad(k, k, k > 1, 1)
            stage_dst(0, 0)
            plan(0, 0, 0, WRITE_QUADS, 0)

            dve.wait_ge(setup_act, 1)
            dve.tensor_scalar(sp0[:, :], sp0[:, :], EXP_CAP, None, ALU.min).then_inc(setup_dve, 1)
            dve.wait_ge(setup_act, 2)
            dve.tensor_tensor(sp0[:, :], sp0[:, :], bo1_c[:, :], ALU.max).then_inc(setup_dve, 1)
            dve.wait_ge(setup_dve, 3)
            dve.tensor_scalar(sp0_shift[:, :], sp0[:, :], -LOG2, None, ALU.add).then_inc(setup_dve, 1)
            dve.wait_ge(setup_dve, 4)
            for v, s0 in enumerate((sp0, sp0_shift)):
                for k in range(KC):
                    ins = dve.tensor_scalar(y_rows[:, k, v * P:(v + 1) * P], ones[:, :], s0[:, k:k + 1], None, ALU.mult)
                ins.then_inc(setup_dve, 1)
            dve.wait_ge(setup_pe, 1)
            dve.wait_ge(weights_in[9], 16)
            dve.tensor_tensor(filt_bias[:, :], ps_f[:, 0, 0:KC], bf2_c[:, :], ALU.add)

            def stream_stats(q, s, h):
                dve.wait_ge(x_loaded[2 * s + h], q * 8 + (16 if s == 0 else 8))
                for a in range(GA):
                    ins = dve.bn_stats(stats[:, s, h * GA + a], xs[:, 2 * s + h, a])
                if h == 1:
                    ins.then_inc(stats_made, 1)

            def edge_stats(q, s):
                dve.wait_ge(gathered[s], q * 32 + (64 if s == 0 else 32))
                for j in range(JT):
                    dve.bn_stats(stats[:, s, 2 * GA + j], xg[:, s, j])

            def small_done(q, n):
                dve.wait_ge(small_step, q * 6 + n)

            def variance_terms(q, s):
                dve.wait_ge(stats_made, q + 1)
                me, mo = stats[:, s, :, 1], stats[:, s, :, 4]
                dve.tensor_tensor(st_a[:, :], me, mo, ALU.subtract).then_inc(small_step, 1)
                dve.tensor_tensor(st_sum[:, :], me, mo, ALU.add)
                dve.tensor_tensor(st_b[:, :], stats[:, s, :, 2], stats[:, s, :, 5], ALU.add).then_inc(small_step, 1)

            def variance_square(q):
                small_done(q, 1)
                dve.scalar_tensor_tensor(out=st_c[:, :], in0=st_a[:, :], scalar=0.25, in1=st_a[:, :],
                                         op0=ALU.mult, op1=ALU.mult).then_inc(small_step, 1)

            def variance(q):
                small_done(q, 3)
                dve.scalar_tensor_tensor(out=st_var[:, :], in0=st_b[:, :], scalar=1.0 / F, in1=st_c[:, :],
                                         op0=ALU.mult, op1=ALU.add).then_inc(var_ready, 1)

            def norm_1(q):
                dve.wait_ge(seed_ready, q + 1)
                dve.scalar_tensor_tensor(out=st_c[:, :], in0=st_var[:, :], scalar=EPS, in1=st_seed[:, :],
                                         op0=ALU.add, op1=ALU.mult).then_inc(small_step, 1)

            def norm_2(q):
                small_done(q, 4)
                dve.scalar_tensor_tensor(out=st_a[:, :], in0=st_c[:, :], scalar=-0.5, in1=st_seed[:, :],
                                         op0=ALU.mult, op1=ALU.mult).then_inc(small_step, 1)

            def norm_3(q, s):
                small_done(q, 5)
                dve.scalar_tensor_tensor(out=rstd[:, s], in0=st_a[:, :], scalar=1.5, in1=st_seed[:, :],
                                         op0=ALU.add, op1=ALU.mult).then_inc(small_step, 1)

            def norm_4(q, s):
                small_done(q, 6)
                dve.scalar_tensor_tensor(out=shift[:, s], in0=st_sum[:, :], scalar=-0.5, in1=rstd[:, s],
                                         op0=ALU.mult, op1=ALU.mult).then_inc(norm_ready, 1)

            stream_stats(0, 0, 0)
            edge_stats(0, 0)
            stream_stats(0, 0, 1)
            variance_terms(0, 0)
            variance_square(0)
            variance(0)
            norm_1(0)
            norm_2(0)
            norm_3(0, 0)
            norm_4(0, 0)

            dve.wait_ge(setup_pe, 2)
            dve.wait_ge(weights_in[11], 16)
            dve.tensor_copy(lean_row[:, :], ps_h[:, 0, 0:F])
            dve.tensor_tensor(lone_row[:, :], ps_h[:, 1, 0:F], bo2_row[:, :], ALU.add).then_inc(setup_done, 1)
            dve.wait_ge(setup_done, 1)
            dve.wait_ge(pre_used, WRITE_QUADS)
            dve.tensor_copy(lone_hi, lone_row[:, :]).then_inc(lone_step, 1)
            dve.wait_ge(lone_step, 1)
            dve.tensor_tensor(lone_rest, lone_row[:, :], lone_hi, ALU.subtract)
            dve.tensor_scalar(lone_sum, lone_hi, ident[:, 0:1], None, ALU.mult).then_inc(lone_step, 1)
            dve.wait_ge(lone_step, 2)
            dve.tensor_copy(lone_mid, lone_rest).then_inc(lone_step, 1)
            dve.wait_ge(lone_step, 3)
            dve.tensor_tensor(lone_low, lone_rest, lone_mid, ALU.subtract).then_inc(lone_step, 1)
            dve.wait_ge(lone_step, 4)
            dve.scalar_tensor_tensor(out=lone_rest, in0=lone_mid, scalar=ident[:, 1:2], in1=lone_sum,
                                     op0=ALU.mult, op1=ALU.add).then_inc(lone_step, 1)
            dve.wait_ge(lone_step, 5)
            for a in range(2):
                ins = dve.scalar_tensor_tensor(out=lone_parts[:, a], in0=lone_low, scalar=ident[:, 2:3], in1=lone_rest,
                                               op0=ALU.mult, op1=ALU.add)
            ins.then_inc(lone_step, 1)
            for n in (2, 8):
                dve.wait_ge(weights_in[n], 16)

            def keep_reps(n, k, times, more=True):
                dve.wait_ge(looked[k], times * (16 * JT))
                ins = dve.tensor_copy(rep_i[:, bass.ds(n * JT, JT)], rep_now[:, k])
                if more:
                    ins = dve.tensor_copy(look_idx[:, k], table_idx[:, bass.ds((n + 3) * JT, JT)])
                ins.then_inc(rep_saved, 1)

            def match(q, s):
                dve.wait_ge(row_loaded[s], q * 8 + (16 if s == 0 else 8))
                if not (isinstance(q, int) and q == 0):
                    dve.wait_ge(merged, q)
                for j in range(JT):
                    w = (j + 1) * P
                    ins = dve.tensor_scalar(same[:, same_at[j]:same_at[j] + w], src_row[:, s, 0:w],
                                            src_f[:, bass.ds(q * JT + j, 1)], weight[:, bass.ds(q * JT + j, 1)],
                                            ALU.is_equal, ALU.mult)
                ins.then_inc(same_ready, 1)

            def message(q):
                dve.wait_ge(filt2_done, q + 1)
                dve.wait_ge(proj_ready, q + 1)
                for k in range(KC):
                    ins = dve.scalar_tensor_tensor(out=msg[:, k], in0=ps_f[:, k], scalar=filt_bias[:, k:k + 1],
                                                   in1=msg[:, k], op0=ALU.add, op1=ALU.mult)
                ins.then_inc(msg_ready, 1)

            def body(q, s, halves, write=(), keep=(), last=False, fetch=True):
                static = isinstance(q, int)

                def combine(b, between=lambda: None):
                    h, a0 = b // 2, (b % 2) * 4
                    out_rows, x_rows = hs[:, h, a0:a0 + 4], xs[:, 2 * s + h, a0:a0 + 4]
                    dve.wait_ge(stream_normed, q * 4 + b + 1)
                    by_tensor, count = halves[b]
                    if by_tensor:
                        dve.wait_ge(x_copied, count)
                        dve.tensor_tensor(flat(out_rows), flat(out_rows), flat(ps_u[:, :, :]), ALU.add
                                          ).then_inc(half_summed, 1)
                        between()
                    else:
                        dve.tensor_tensor(flat(out_rows), flat(out_rows), flat(x_rows), ALU.add).then_inc(x_added, 1)
                        between()
                        dve.wait_ge(x_added, count)
                        dve.tensor_tensor(out_rows, out_rows, lone_row[:, :].unsqueeze(1).broadcast_to([P, 4, F]),
                                          ALU.add).then_inc(half_summed, 1)

                if not static or q > 0:
                    match(q - 1, 1 - s)
                if not last:
                    stream_stats(q + 1, 1 - s, 0)
                combine(0)
                if not static or q > 0:
                    message(q - 1)
                if not last:
                    edge_stats(q + 1, 1 - s)
                combine(1)
                dve.wait_ge(exp_done, q + 1)
                dve.tensor_scalar(flat(soft[:, :, :]), flat(soft[:, :, :]), EXP_CAP, None, ALU.min).then_inc(capped, 1)
                if not last:
                    stream_stats(q + 1, 1 - s, 1)
                    if fetch:
                        ins = stage_dst(q + 1, 1 - s)
                        if not write:
                            ins.then_inc(staged, 1)
                    variance_terms(q + 1, 1 - s)
                dve.wait_ge(log_done, q + 1)
                for k in range(KC):
                    ins = dve.scalar_tensor_tensor(out=soft[:, k], in0=ps_a[:, k], scalar=bf1_c[:, k:k + 1],
                                                   in1=soft[:, k], op0=ALU.add, op1=ALU.max)
                    if k == KC - 1:
                        ins.then_inc(soft_ready, 1)
                    if not last:
                        (variance_square, variance)[k](q + 1)
                if write:
                    n, count, loads, written = write
                    for k in range(count):
                        cover_quad(n + k, k, True, loads if k == 2 else q + 2)
                    plan(q + 1, 1 - s, n, count, written)
                combine(2)
                for n, k, times in keep:
                    keep_reps(n, k, times, more=not (isinstance(n, int) and n >= QUADS - 3))
                if last:
                    combine(3)
                else:
                    norm_1(q + 1)
                    norm_2(q + 1)
                    norm_3(q + 1, 1 - s)
                    combine(3, lambda: norm_4(q + 1, 1 - s))

            def early_copies(q):
                return (True, q * 3 + 1), (True, q * 3 + 2), (True, q * 3 + 3), (False, q + 1)

            def even_copies(r):
                copied, added_to = (r - E2) * 3 + EARLY * 3, (r - E2) * 5 + EARLY
                return (False, added_to + 1), (False, added_to + 2), (True, copied + 1), (False, added_to + 3)

            def odd_copies(r):
                copied, added_to = (r - E2) * 3 + EARLY * 3 + 1, (r - E2) * 5 + EARLY + 3
                return (False, added_to + 1), (True, copied + 1), (True, copied + 2), (False, added_to + 2)

            def write_odd(r):
                return r * 5 + 3, 2, None, r * 5

            def write_even(r):
                return r * 5 + 5, 3, r + 2, r * 5 + 3

            body(0, 0, early_copies(0), write_odd(0))
            body(1, 1, early_copies(1), write_even(0))
            with dve.Fori(1, E2 - 2) as r:
                body(r * 2, 0, early_copies(r * 2), write_odd(r))
                body(r * 2 + 1, 1, early_copies(r * 2 + 1), write_even(r))
            body(16, 0, early_copies(16), write_odd(8))
            body(17, 1, early_copies(17), (45, 2, None, 43))
            body(18, 0, early_copies(18), (47, 2, None, 45))
            body(19, 1, early_copies(19))
            body(20, 0, even_copies(10), keep=((0, 0, 1),))
            body(21, 1, odd_copies(10), keep=((1, 1, 1), (2, 2, 1)))
            with dve.Fori(E2 + 1, FAST // 2) as r:
                body(r * 2, 0, even_copies(r), keep=(((r - E2) * 3, 0, r - E2 + 1),))
                body(r * 2 + 1, 1, odd_copies(r), keep=(((r - E2) * 3 + 1, 1, r - E2 + 1), ((r - E2) * 3 + 2, 2, r - E2 + 1)))
            for q in range(FAST, QUADS):
                n = (q - FAST) * 2 + FAST_FROM
                body(q, q % 2, (even_copies, odd_copies)[q % 2](q // 2),
                     keep=[(m, m % 3, m // 3 + 1) for m in (n, n + 1)], last=(q == QUADS - 1), fetch=(q < QUADS - 3))
            match(QUADS - 1, 0)
            message(QUADS - 1)
            for n in range(AFTER, QUADS):
                keep_reps(n, n % 3, n // 3 + 1, more=False)

            whole = TILES // 8 * 8

            def with_spares(o, i, op):
                dve.tensor_tensor(o[:, 0:whole].rearrange("p (a b) -> p a b", b=8),
                                  i[:, 0:whole].rearrange("p (a b) -> p a b", b=8),
                                  trash_i[:, :].unsqueeze(1).broadcast_to([P, TILES // 8, 8]), op)
                return dve.tensor_tensor(o[:, whole:TILES], i[:, whole:TILES], trash_i[:, 0:TILES - whole], op)

            dve.wait_ge(y_done, QUADS)
            dve.wait_ge(rep_saved, QUADS)
            is_rep, gain = msg[:, 0, 0:TILES], msg[:, 1, 0:TILES]
            dve.tensor_tensor(is_rep, rep_i[:, :], edge_i[:, :], ALU.is_equal)
            with_spares(gain, src_f, ALU.subtract).then_inc(out_idx_step, 1)
            dve.wait_ge(out_idx_step, 1)
            dve.tensor_tensor(gain, gain, is_rep, ALU.mult).then_inc(out_idx_step, 1)
            dve.wait_ge(out_idx_step, 2)
            with_spares(out_idx, gain, ALU.add).then_inc(out_idx_made, 1)
            dve.wait_ge(out_idx_made, 1)

            def f_cap(q, s):
                dve.wait_ge(f_exp, q + 1)
                e = flat(ring[:, 2 + s])
                dve.tensor_scalar(e, e, EXP_CAP, None, ALU.min).then_inc(f_capped, 1)

            def f_max(q, s, wait=True):
                dve.wait_ge(f_log, q + 1)
                if wait:
                    dve.wait_ge(f_out, q - 1)
                for k in range(KC):
                    half = bass.ts(k, QE)
                    ins = dve.scalar_tensor_tensor(out=flat(ring[:, 6 + s])[:, half], in0=(ps_f, ps_h)[s][:, k],
                                                   scalar=bo1_c[:, k:k + 1], in1=flat(ring[:, 2 + s])[:, half],
                                                   op0=ALU.add, op1=ALU.max)
                ins.then_inc(f_soft, 1)

            def f_sub(q, s, wait=True):
                dve.wait_ge(f_out, q + 1)
                if wait:
                    dve.wait_ge(out_added[s], (q - s) * 32)
                dve.tensor_copy(dst_now[:, s], out_idx[:, bass.ds(q * JT, JT)])
                rows = (ps_a, ps_u)[s][:, :, :].rearrange("p k (a f) -> p (k a) f", f=F)
                dve.tensor_tensor(ring[:, 4 + s], rows, lean_row[:, :].unsqueeze(1).broadcast_to([P, JT, F]),
                                  ALU.subtract).then_inc(f_rows, 1)

            f_cap(0, 0)
            f_cap(1, 1)
            f_max(0, 0, False)
            f_max(1, 1, False)
            f_cap(2, 0)
            f_sub(0, 0, False)
            f_max(2, 0)
            f_cap(3, 1)
            f_sub(1, 1, False)
            f_max(3, 1)
            with dve.Fori(2, QUADS // 2) as r:
                f_cap(r * 2, 0)
                f_sub(r * 2 - 2, 0)
                f_max(r * 2, 0)
                f_cap(r * 2 + 1, 1)
                f_sub(r * 2 - 1, 1)
                f_max(r * 2 + 1, 1)
            f_cap(QUADS - 1, 0)
            f_sub(QUADS - 3, 0)
            f_max(QUADS - 1, 0)
            f_sub(QUADS - 2, 1)
            f_sub(QUADS - 1, 0)


def kernel(**inputs):
    import numpy as np
    import concourse.bacc as bacc
    from concourse import mybir as mb
    from concourse.bass_utils import run_bass_kernel_spmd as run

    nc = bacc.Bacc("TRN2", target_bir_lowering=False, num_devices=1)
    a = {k: np.asarray(v) for k, v in inputs.items()}

    def padded(v, fill):
        return np.concatenate([v, np.full((PAD_EDGES - EDGES,) + v.shape[1:], fill, v.dtype)])

    def cols(v, fill):
        return np.ascontiguousarray(padded(v, fill).reshape(QUADS, P, JT).transpose(1, 0, 2).reshape(P, TILES))

    def by_tile(v, fill):
        v = padded(v, fill)
        return v.reshape((QUADS, P, JT) + v.shape[1:]).swapaxes(1, 2).reshape((QUADS, QE) + v.shape[1:])

    def chunked(v):
        return np.ascontiguousarray(v.reshape(KC, P).T)

    arrays = {
        "x": np.ascontiguousarray(a["x"]),
        "src_cols": cols(a["src"], ATOMS),
        "src_rows": np.ascontiguousarray(by_tile(a["src"], ATOMS)),
        "dst_cols": cols(a["dst"], 0),
        "attr_t": np.ascontiguousarray(by_tile(a["edge_attr_64"], 0).reshape(PAD_EDGES, R).T),
        "weight_cols": cols(a["edge_weight1"][:, 0], 0),
        "w_in": a["L0_gnn_W_in2f"], "wf1": a["L0_gnn_Wf1"], "bf1": chunked(a["L0_gnn_bf1"]),
        "wf2": a["L0_gnn_Wf2"], "bf2": chunked(a["L0_gnn_bf2"]), "wo1": a["L0_gnn_Wo1"],
        "bo1": chunked(a["L0_gnn_bo1"]), "wo2": a["L0_gnn_Wo2"], "bo2": a["L0_gnn_bo2"].reshape(1, F),
    }
    feeds = {f"in_{k}": np.ascontiguousarray(v) for k, v in arrays.items()}
    args = [nc.dram_tensor(k, v.shape, mb.dt.from_np(v.dtype), kind="ExternalInput").ap() for k, v in feeds.items()]
    out = nc.dram_tensor("out_rows", (OUT_ROWS, F), mb.dt.float32, kind="ExternalOutput").ap()
    build(nc, *args, out)
    r = run(nc, [feeds], core_ids=[0])
    return r.results[0]["out_rows"][:ATOMS]
```
